# Optimizing a Trainium2 kernel written in Bass

```python
import numpy as np
import jax
import jax.numpy as jnp

def _softmax(x, axis=-1):
    return jax.nn.softmax(x, axis=axis)

def _gelu(x):
    return jax.nn.gelu(x, approximate=True)

def _silu(x):
    return jax.nn.silu(x)

def _sigmoid(x):
    return jax.nn.sigmoid(x)

def _layernorm(x, axis=-1, eps=1e-05):
    m = jnp.mean(x, axis=axis, keepdims=True)
    v = jnp.var(x, axis=axis, keepdims=True)
    return (x - m) / jnp.sqrt(v + eps)

def _scatter_add(tgt, idx, src, axis=0):
    return tgt.at[idx].add(src)

def _segment_sum(src, seg, n):
    return jax.ops.segment_sum(src, seg, n)
kernel_name = 'mk_adj_preln_d2_adj_r2_b308f9'

def setup_inputs(seed: int=0):
    np.random.seed(seed)
    _w = jnp.asarray

    def _rec_inputs():
        import jax
        import jax.numpy as jnp
        _gk = jax.random.key(seed)
        x = -0.000929 + 1 * jax.random.normal(jax.random.fold_in(_gk, 1), (8, 2048, 64), jnp.float32)
        _a = jax.random.bernoulli(jax.random.fold_in(_gk, 2), 0.00195312, (8, 2048, 2048))
        _a = jnp.logical_or(_a, jnp.swapaxes(_a, -1, -2))
        _a = jnp.logical_or(_a, jnp.eye(2048, dtype=bool))
        _af = _a.astype(jnp.float32)
        _af = _af * jax.random.uniform(jax.random.fold_in(_gk, 3), (8, 2048, 2048), jnp.float32, 0.05, 1)
        adj = _af
        return (x, adj)
    x, adj = _rec_inputs()

    def _L0_gnn_setup():
        import jax, jax.numpy as jnp
        import numpy as np
        B, N, C, R = (4, 2048, 64, 16)
        EPS = 1e-12
        key = jax.random.key(seed)
        k_x, k_w, k_u = jax.random.split(key, 3)
        x = jax.random.normal(k_x, (B, N, C), dtype=jnp.float32)
        W = jax.random.uniform(k_w, (B, N, N), dtype=jnp.float32)
        U = 0.01 * jax.random.normal(k_u, (N, R), dtype=jnp.float32)
        w_scale = jnp.asarray(1.0, dtype=jnp.float32)
        return {'x': x, 'W': W, 'U': U, 'w_scale': w_scale}
    _L0_gnn_all = _L0_gnn_setup()
    _L0_gnn_in = {k: v for k, v in _L0_gnn_all.items() if k in ('U', 'w_scale')}
    del _L0_gnn_all

    def _L1_gnn_setup():
        import jax, jax.numpy as jnp
        import numpy as np
        B, N, F_IN, F_OUT = (4, 2048, 64, 64)
        ALPHA = 0.2
        M_MIX = 0.8
        NEG_INF = -1000000000000.0
        key = jax.random.key(seed)
        k1, k2, k3, k4 = jax.random.split(key, 4)
        inp = jax.random.normal(k1, (B, N, F_IN), dtype=jnp.float32)
        adj = jax.random.uniform(k2, (B, N, N), dtype=jnp.float32)
        limW = 1.414 * np.sqrt(6.0 / (F_IN + F_OUT))
        W = jax.random.uniform(k3, (F_IN, F_OUT), dtype=jnp.float32, minval=-limW, maxval=limW)
        lima = 1.414 * np.sqrt(6.0 / (2 * F_OUT + 1))
        a = jax.random.uniform(k4, (2 * F_OUT, 1), dtype=jnp.float32, minval=-lima, maxval=lima)
        return {'inp': inp, 'adj': adj, 'W': W, 'a': a}
    _L1_gnn_all = _L1_gnn_setup()
    _L1_gnn_in = {k: v for k, v in _L1_gnn_all.items() if k in ('W', 'a')}
    del _L1_gnn_all
    return {'x': x, 'adj': adj, 'L0_gnn_U': _L0_gnn_in['U'], 'L0_gnn_w_scale': _L0_gnn_in['w_scale'], 'L1_gnn_W': _L1_gnn_in['W'], 'L1_gnn_a': _L1_gnn_in['a']}

def reference(x, adj, L0_gnn_U, L0_gnn_w_scale, L1_gnn_W, L1_gnn_a):
    import jax
    import jax.numpy as jnp

    def _L0_gnn_ref(x, W, U, w_scale):
        import jax, jax.numpy as jnp
        import numpy as np
        B, N, C, R = (4, 2048, 64, 16)
        EPS = 1e-12
        Ws = 0.5 * (W + jnp.swapaxes(W, -1, -2))
        A = jax.nn.sigmoid(U @ U.T)
        K = Ws * A[None, :, :]
        deg = jnp.maximum(K.sum(axis=-1), EPS)
        d = jax.lax.rsqrt(deg)
        K = K * d[:, :, None] * d[:, None, :]
        return w_scale * jnp.einsum('bnm,bmc->bnc', K, x)

    def _L1_gnn_ref(inp, adj, W, a):
        import jax, jax.numpy as jnp
        import numpy as np
        B, N, F_IN, F_OUT = (4, 2048, 64, 64)
        ALPHA = 0.2
        M_MIX = 0.8
        NEG_INF = -1000000000000.0
        h = jnp.einsum('bnf,fo->bno', inp, W)
        lh = jax.nn.leaky_relu(h, negative_slope=ALPHA)
        f_src = lh @ a[:F_OUT, 0]
        f_dst = lh @ a[F_OUT:, 0]
        e = f_src[:, :, None] + f_dst[:, None, :]
        dj = M_MIX * adj + (1.0 - M_MIX) * e
        attention = jnp.where(dj > 0, dj, NEG_INF)
        attention = jax.nn.softmax(attention, axis=1)
        h_prime = jnp.einsum('bij,bjo->bio', attention, h)
        return jax.nn.relu(h_prime)
    h = jnp.maximum(_layernorm(x, axis=-1), 0.0)
    x = x + _L0_gnn_ref(h, adj, L0_gnn_U, L0_gnn_w_scale)
    h = jnp.maximum(_layernorm(x, axis=-1), 0.0)
    x = x + _L1_gnn_ref(h, adj, L1_gnn_W, L1_gnn_a)
    return x

_drawn_inputs = setup_inputs


def setup_inputs(seed=0):
    import zlib

    import numpy as np

    out = dict(_drawn_inputs(seed))
    spreads = {}
    factors = {'L0_gnn_U': 64.0}
    for name, (base, spread) in spreads.items():
        noise = np.random.default_rng([zlib.crc32(name.encode()), seed]).standard_normal(out[name].shape)
        drawn = base * np.exp(spread * noise) if base else spread * noise
        out[name] = jnp.asarray(drawn.astype(out[name].dtype))
    for name, factor in factors.items():
        out[name] = (out[name] * factor).astype(out[name].dtype)
    return out
```

```python
from contextlib import ExitStack

import numpy as np
import concourse.bass as bass
from concourse import mybir

F32 = mybir.dt.float32
ALU = mybir.AluOpType
ACT = mybir.ActivationFunctionType
AX_X = mybir.AxisListType.X

P = 128
BATCH, NODES, CH, RANK = 8, 2048, 64, 16
TILES = NODES // P
ROW = TILES * CH
CHUNK = 512
CHUNKS = NODES // CHUNK
HALF = ROW // 2

UNIT = 8
UNITS = [(r, c, min(c + UNIT, TILES)) for r in range(TILES) for c in range(r, TILES, UNIT)]
UNITS_OF = [[n for n, (row, _, _) in enumerate(UNITS) if row == r] for r in range(TILES)]
PAIR_SLOTS = 3
ADJT_SLOTS = 4
assert len(UNITS) % PAIR_SLOTS == 0 and TILES % ADJT_SLOTS == 0
PAIR_AT = np.cumsum([0] + [2 * (c1 - c0) * P for _, c0, c1 in UNITS]).tolist()
PAIR_ROW = PAIR_AT[-1]

GATE_AT = np.cumsum([0] + [(TILES - r) * P for r in range(TILES)]).tolist()
K_AT = GATE_AT[:8] * 2
K_ROW = GATE_AT[8]
LEFT_AT = [0, (TILES - 2) * P]
LEFT_ROW = LEFT_AT[1] + (TILES - 1) * P
AGG_T, ACTIV_T, LEAKY_T = 0, ROW, 2 * ROW

TURNS = [-(-r // 4) for r in range(TILES)]
TURN_AT = np.cumsum([0] + TURNS).tolist()
W_AGG = TURN_AT[-1]
W_XN = W_AGG + 2
W_HID = W_XN + 2
W_SRC = W_HID + 2
W_DST = W_SRC + 4
W_NAT = W_DST + 2
W_OUT = W_NAT + 2
W_STEP = W_STEP_END = W_OUT + 2
GATE_TURNS_BY = np.cumsum([-(-(TILES - r) // 4) for r in range(TILES)]).tolist()
W_GATES = sum(-(-(TILES - r) // 4) for r in range(TILES))
assert W_GATES % 2 == 0 and W_STEP % 2 == 0

ROWS_AT = {1: [0], 2: [1], 3: [2, 3], 4: [4, 5], 5: [6, 7], 6: [8, 9], 7: [10, 11], 8: [12, 13],
           9: [14, 15], 10: [16]}
J_AGG, J_X1, J_CENTER, J_NORM, J_NEXT = 11, 12, 13, 14, 14

C_ID, C_W, C_SRC, C_DST, C_SCALE = 0, P, 2 * P, 4 * P, 4 * P + 2
C_COLS = C_SCALE + 1


def work_base(b):
    return W_GATES if isinstance(b, int) and b == 0 else W_GATES + W_OUT + W_STEP * (b - 1)


def gnn_program(nc, x, pairs, adj_t, u_t, consts, out):
    with ExitStack() as ctx:
        def sb(name, cols, parts=P):
            return ctx.enter_context(nc.sbuf_tensor(name, [parts, cols], F32))

        def sem(name):
            return ctx.enter_context(nc.semaphore(name))

        gate = sb("gate", GATE_AT[-1])
        k_rows = sb("k_rows", K_ROW)
        left = sb("left", LEFT_ROW)
        pair = [sb(f"pair{i}", 2 * UNIT * P) for i in range(PAIR_SLOTS)]
        adjt = [sb(f"adjt{i}", NODES) for i in range(ADJT_SLOTS)]
        src_row = sb("src_row", NODES)
        x_in = sb("x_in", ROW)
        x_norm = sb("x_norm", ROW)
        x1_next = sb("x1_next", ROW)
        x1 = sb("x1", ROW)
        hidden = sb("hidden", ROW)
        cst = sb("cst", C_COLS)
        scaled = [sb(f"scaled{i}", CH) for i in range(2)]
        weighed = [sb(f"weighed{i}", CH) for i in range(2)]
        deg_part = sb("deg_part", TILES * 6)
        deg = sb("deg", TILES)
        deg_inv = sb("deg_inv", TILES)
        deg_out = sb("deg_out", TILES)
        minus_half = sb("minus_half", TILES)
        ln_mean = sb("ln_mean", TILES)
        ln_var = sb("ln_var", TILES)
        low = sb("low", TILES)
        dst = sb("dst", TILES)
        flag = sb("flag", TILES)
        part_sum = sb("part_sum", TILES * 4)
        total = sb("total", TILES)
        lone_sum = sb("lone_sum", CH)
        uniform = sb("uniform", 1)
        u_sb = src_row[0:RANK, :]

        acc0 = ctx.enter_context(nc.psum_tensor("acc0", [P, 2 * CHUNK], F32))
        acc1 = ctx.enter_context(nc.psum_tensor("acc1", [P, 2 * CHUNK], F32))
        exps = ctx.enter_context(nc.psum_tensor("exps", [P, 2 * CHUNK], F32))
        work = ctx.enter_context(nc.psum_tensor("work", [P, 2 * CHUNK], F32))

        s_cst = sem("consts_loaded")
        s_u = sem("u_loaded")
        s_pair = [sem(f"pair_loaded{i}") for i in range(PAIR_SLOTS)]
        s_adjt = [sem(f"adjt_loaded{i}") for i in range(ADJT_SLOTS)]
        s_x = sem("x_loaded")
        s_stored = sem("out_stored")
        s_const = sem("small_consts_set")
        s_filled = sem("work_filled")
        s_drained = sem("work_drained")
        s_sum = sem("pairs_summed")
        s_k = sem("k_units_made")
        s_degp = sem("degrees_summed")
        s_degc = sem("degrees_clamped")
        s_deg = sem("degrees_inverted")
        s_scaled = sem("scaled_rows_made")
        s_mm0 = sem("layer0_rows_multiplied")
        s_agg = sem("agg_copied")
        s_dw = sem("deg_out_made")
        s_aggs = sem("agg_scaled")
        s_x1 = sem("x1_made")
        s_x1m = sem("x1_moved")
        s_lsum = sem("ln_summed")
        s_mean = sem("ln_mean_made")
        s_cent = sem("ln_centered")
        s_sq = sem("ln_squared")
        s_vsum = sem("ln_squares_summed")
        s_var = sem("ln_var_made")
        s_rstd = sem("ln_rstd_made")
        s_norm = sem("ln_normed")
        s_leaky = sem("leaky_made")
        s_begun = sem("logits_begun")
        s_t = sem("logits_made")
        s_e = sem("exp_chunks_made")
        s_p = sem("masked_chunks_made")
        s_z1 = sem("totals_summed")
        s_z2 = sem("totals_clamped")
        s_z = sem("totals_inverted")
        s_hz = sem("weighed_rows_made")
        s_mm1 = sem("layer1_rows_multiplied")
        s_flag = sem("lone_flags_made")
        s_lone = sem("lone_hidden_made")
        s_lsm = sem("lone_sum_made")
        s_acc1 = sem("acc1_complete")
        s_hpt = sem("acc1_copied")
        s_out = sem("out_made")

        ident = cst[:, C_ID:C_ID + P]
        w_pair = cst[:, C_W:C_W + P]

        def bank(n):
            return work[:, (n % 2) * CHUNK:(n % 2 + 1) * CHUNK]

        def tch(ap):
            return ap.rearrange("p (t c) -> p t c", c=CH)

        def per_tile(col):
            return col[:, :].unsqueeze(2).to_broadcast([P, TILES, CH])

        def chunk_of(acc, q):
            return acc[CH * (q % 2):CH * (q % 2) + CH, (q // 2) * CHUNK:(q // 2 + 1) * CHUNK]

        block = ctx.enter_context(nc.Block())

        @block.sync
        def _(sp):
            def load_pair(b, n):
                sp.dma_start(pair[n % PAIR_SLOTS][:, 0:PAIR_AT[n + 1] - PAIR_AT[n]],
                             pairs[b, :, PAIR_AT[n]:PAIR_AT[n + 1]]).then_inc(s_pair[n % PAIR_SLOTS], 16)

            def load_pair_behind(b, n):
                sp.wait_ge(s_k, len(UNITS) * b + n + 1)
                if n + PAIR_SLOTS < len(UNITS):
                    load_pair(b, n + PAIR_SLOTS)
                else:
                    load_pair(b + 1, n + PAIR_SLOTS - len(UNITS))

            def load_adjt(b, j):
                sp.dma_start(adjt[j % ADJT_SLOTS][:, :], adj_t[b, j, :, :]).then_inc(s_adjt[j % ADJT_SLOTS], 16)

            def load_adjt_behind(b, j, last):
                nxt = j + ADJT_SLOTS
                if nxt < TILES:
                    sp.wait_ge(s_mm1, TILES * b + j + 1)
                    load_adjt(b, nxt)
                elif not last:
                    sp.wait_ge(s_mm1, TILES * b + j + 1)
                    load_adjt(b + 1, nxt - TILES)

            def load_x(b):
                sp.dma_start(x_in[:, :], x[b, :, :]).then_inc(s_x, 16)

            def step(b, l0, more):
                for j in range(1, TILES):
                    if l0:
                        for r in ROWS_AT.get(j, []):
                            for n in UNITS_OF[r] if r < TILES else []:
                                if more or n + PAIR_SLOTS < len(UNITS):
                                    load_pair_behind(b + 1, n)
                        if j == J_CENTER and more:
                            sp.wait_ge(s_x1, b + 2)
                            load_x(b + 2)
                    if j >= 2:
                        load_adjt_behind(b, j - 2, not l0)
                load_adjt_behind(b, TILES - 2, not l0)
                sp.wait_ge(s_out, b + 1)
                sp.dma_start(out[b, :, :], left[:, AGG_T:AGG_T + ROW]).then_inc(s_stored, 16)
                sp.wait_ge(s_stored, 16 * (b + 1))
                if l0:
                    load_adjt(b + 1, ADJT_SLOTS - 1)

            sp.dma_start(u_sb, u_t[:, :]).then_inc(s_u, 16)
            load_pair(0, 0)
            sp.dma_start(cst[:, :], consts[:, :]).then_inc(s_cst, 16)
            load_x(0)
            for n in range(1, PAIR_SLOTS):
                load_pair(0, n)
            for j in range(ADJT_SLOTS):
                load_adjt(0, j)
            for n in range(len(UNITS)):
                load_pair_behind(0, n)
            sp.wait_ge(s_x1, 1)
            load_x(1)
            with sp.Fori(0, BATCH - 2) as b:
                step(b, True, True)
            step(BATCH - 2, True, False)
            step(BATCH - 1, False, False)

        @block.gpsimd
        def _(pool):
            def sum_pair(b, n):
                pool.wait_ge(s_pair[n % PAIR_SLOTS], 16 * (len(UNITS) // PAIR_SLOTS * b + n // PAIR_SLOTS + 1))
                w = (PAIR_AT[n + 1] - PAIR_AT[n]) // 2
                p = pair[n % PAIR_SLOTS]
                nc.gpsimd.tensor_tensor(p[:, 0:w], p[:, 0:w], p[:, w:2 * w], ALU.add).then_inc(s_sum, 1)

            def invert_degree(b, r):
                pool.wait_ge(s_degc, TILES * b + r + 1)
                nc.gpsimd.tensor_tensor(deg_inv[:, r:r + 1], deg[:, r:r + 1], minus_half[:, r:r + 1],
                                        ALU.pow).then_inc(s_deg, 1)

            def row(b, r, more=True):
                units = UNITS_OF[r + 1] if r + 1 < TILES else []
                if units:
                    sum_pair(b, units[0])
                if r >= 1:
                    invert_degree(b, r - 1)
                for n in units[1:]:
                    sum_pair(b, n)

            def add_layer0(b):
                pool.wait_ge(s_deg, TILES * (b + 1))
                nc.gpsimd.tensor_tensor(deg_out[:, :], deg_inv[:, :],
                                        cst[:, C_SCALE:C_SCALE + 1].to_broadcast([P, TILES]), ALU.mult).then_inc(s_dw, 1)
                pool.wait_ge(s_dw, b + 1)
                pool.wait_ge(s_drained, work_base(b) + W_AGG + 2)
                nc.gpsimd.tensor_tensor(tch(x_norm[:, :]), tch(x_norm[:, :]), per_tile(deg_out),
                                        ALU.mult).then_inc(s_aggs, 1)
                pool.wait_ge(s_aggs, b + 1)
                if not (isinstance(b, int) and b == 0):
                    pool.wait_ge(s_x1m, b)
                nc.gpsimd.tensor_tensor(x1_next[:, :], x_norm[:, :], x_in[:, :], ALU.add).then_inc(s_x1, 1)

            def center(n, source):
                pool.wait_ge(s_mean, n + 1)
                nc.gpsimd.tensor_tensor(tch(x_norm[:, :]), tch(source[:, :]), per_tile(ln_mean),
                                        ALU.subtract).then_inc(s_cent, 1)

            def normalize(n):
                pool.wait_ge(s_var, n + 1)
                nc.gpsimd.tensor_tensor(ln_var[:, :], ln_var[:, :], minus_half[:, :], ALU.pow).then_inc(s_rstd, 1)
                pool.wait_ge(s_rstd, n + 1)
                nc.gpsimd.tensor_tensor(tch(x_norm[:, :]), tch(x_norm[:, :]), per_tile(ln_var),
                                        ALU.mult).then_inc(s_norm, 1)

            def lone(b):
                pool.wait_ge(s_flag, b + 1)
                pool.wait_ge(s_hz, TILES * (b + 1))
                nc.gpsimd.tensor_tensor(tch(hidden[:, :]), tch(hidden[:, :]), per_tile(flag),
                                        ALU.mult).then_inc(s_lone, 1)

            def add_layer1(b, relu_at):
                pool.wait_ge(s_drained, relu_at)
                res = left[:, AGG_T:AGG_T + ROW]
                nc.gpsimd.tensor_tensor(res, res, x1[:, :], ALU.add).then_inc(s_out, 1)

            def step(b, l0, more):
                for j in range(1, TILES):
                    if l0:
                        for r in ROWS_AT.get(j, []):
                            row(b + 1, r)
                        if j == J_X1:
                            add_layer0(b + 1)
                        if j == J_CENTER:
                            center(2 * (b + 1) + 1, x1_next)
                        if j == J_NORM:
                            normalize(2 * (b + 1) + 1)
                if more:
                    pool.wait_ge(s_filled, work_base(b + 1) + W_XN + 2)
                    center(2 * (b + 2), x_in)
                    for n in UNITS_OF[0]:
                        sum_pair(b + 2, n)
                lone(b)
                if more:
                    normalize(2 * (b + 2))
                add_layer1(b, work_base(b + 1) + (W_STEP_END if l0 else 2))

            nc.gpsimd.memset(minus_half[:, :], -0.5).then_inc(s_const, 1)
            pool.wait_ge(s_const, 1)
            center(0, x_in)
            for n in UNITS_OF[0]:
                sum_pair(0, n)
            normalize(0)
            for r in range(TILES + 1):
                row(0, r)
            pool.wait_ge(s_cst, 16)
            add_layer0(0)
            center(1, x1_next)
            normalize(1)
            pool.wait_ge(s_filled, work_base(0) + W_XN + 2)
            center(2, x_in)
            for n in UNITS_OF[0]:
                sum_pair(1, n)
            normalize(2)
            with pool.Fori(0, BATCH - 2) as b:
                step(b, True, True)
            step(BATCH - 2, True, False)
            step(BATCH - 1, False, False)

        @block.vector
        def _(dve):
            def k_unit(b, n):
                r, c0, c1 = UNITS[n]
                dve.wait_ge(s_sum, len(UNITS) * b + n + 1)
                if isinstance(b, int) and b == 0:
                    dve.wait_ge(s_drained, GATE_TURNS_BY[r])
                if r >= UNIT:
                    dve.wait_ge(s_mm0, TILES * b + max(UNIT - 1, r - UNIT + 1))
                elif n == 0 and not (isinstance(b, int) and b == 0):
                    dve.wait_ge(s_mm0, TILES * b)
                at, w = (c0 - r) * P, (c1 - c0) * P
                col = 6 * r + (1 if r >= UNIT or c0 > r else 0)
                nc.vector.tensor_tensor_reduce(k_rows[:, K_AT[r] + at:K_AT[r] + at + w],
                                               pair[n % PAIR_SLOTS][:, 0:w],
                                               gate[:, GATE_AT[r] + at:GATE_AT[r] + at + w],
                                               0.5, 0.0, ALU.mult, ALU.add,
                                               deg_part[:, col:col + 1]).then_inc(s_k, 1)

            def degree(b, r):
                if r >= 1:
                    dve.wait_ge(s_drained, work_base(b) + TURN_AT[r] + TURNS[r])
                dve.wait_ge(s_k, len(UNITS) * b + UNITS_OF[r][-1] + 1)
                first = 6 * r + (1 if r >= UNIT else 0)
                nc.vector.tensor_reduce(deg[:, r:r + 1], deg_part[:, first:6 * r + 2 + TURNS[r]], AX_X,
                                        ALU.add).then_inc(s_degp, 1)
                dve.wait_ge(s_degp, TILES * b + r + 1)
                nc.vector.tensor_scalar(deg[:, r:r + 1], deg[:, r:r + 1], 1e-12, None, ALU.max).then_inc(s_degc, 1)

            def row(b, r):
                if r < TILES:
                    for n in UNITS_OF[r]:
                        k_unit(b, n)
                if r >= 1:
                    degree(b, r - 1)

            def mean(n, source):
                nc.vector.tensor_reduce(ln_mean[:, :], tch(source[:, :]), AX_X, ALU.add).then_inc(s_lsum, 1)
                dve.wait_ge(s_lsum, n + 1)
                nc.vector.tensor_scalar(ln_mean[:, :], ln_mean[:, :], 1.0 / CH, None, ALU.mult).then_inc(s_mean, 1)

            def variance(n):
                dve.wait_ge(s_sq, n + 1)
                nc.vector.tensor_reduce(ln_var[:, :], tch(left[:, AGG_T:AGG_T + ROW]), AX_X, ALU.add).then_inc(s_vsum, 1)
                dve.wait_ge(s_vsum, n + 1)
                nc.vector.tensor_scalar(ln_var[:, :], ln_var[:, :], 1.0 / CH, 1e-5, ALU.mult, ALU.add).then_inc(s_var, 1)

            def logits(b, j):
                dve.wait_ge(s_adjt[j % ADJT_SLOTS], 16 * (TILES // ADJT_SLOTS * b + j // ADJT_SLOTS + 1))
                if j == 0:
                    dve.wait_ge(s_drained, work_base(b) + W_SRC + 4)
                dve.sem_inc(s_begun, 1)
                a = adjt[j % ADJT_SLOTS][:, :]
                nc.vector.tensor_tensor_reduce(a, a, src_row[:, :], -0.8, 3.0e38, ALU.add, ALU.min,
                                               low[:, j:j + 1]).then_inc(s_t, 1)

            def masked(b, j):
                if j == 0:
                    dve.wait_ge(s_drained, work_base(b) + W_DST + 2)
                for q in range(CHUNKS):
                    dve.wait_ge(s_e, CHUNKS * (TILES * b + j) + q + 1)
                    a = adjt[j % ADJT_SLOTS][:, q * CHUNK:(q + 1) * CHUNK]
                    nc.vector.scalar_tensor_tensor(a, a, dst[:, j:j + 1], exps[:, (q % 2) * CHUNK:(q % 2 + 1) * CHUNK],
                                                   ALU.is_lt, ALU.mult,
                                                   part_sum[:, 4 * j + q:4 * j + q + 1]).then_inc(s_p, 1)

            def total1(b, j):
                dve.wait_ge(s_p, CHUNKS * (TILES * b + j + 1))
                nc.vector.tensor_reduce(total[:, j:j + 1], part_sum[:, 4 * j:4 * j + 4], AX_X, ALU.add).then_inc(s_z1, 1)

            def total2(b, j):
                dve.wait_ge(s_z1, TILES * b + j + 1)
                nc.vector.tensor_scalar(total[:, j:j + 1], total[:, j:j + 1], 0.5, None, ALU.max).then_inc(s_z2, 1)

            def total3(b, j):
                dve.wait_ge(s_z2, TILES * b + j + 1)
                nc.vector.reciprocal(total[:, j:j + 1], total[:, j:j + 1]).then_inc(s_z, 1)

            def leaky(b):
                dve.wait_ge(s_drained, work_base(b) + W_HID + 2)
                h = left[:, LEAKY_T:LEAKY_T + ROW]
                nc.vector.scalar_tensor_tensor(h, h, 0.2, h, ALU.mult, ALU.max).then_inc(s_leaky, 1)

            def flags(b):
                dve.wait_ge(s_t, TILES * (b + 1))
                nc.vector.tensor_tensor(flag[:, :], low[:, :], dst[:, :], ALU.is_ge).then_inc(s_flag, 1)

            def lone_sums(b):
                dve.wait_ge(s_lone, b + 1)
                nc.vector.tensor_reduce(lone_sum[:, :], hidden[:, :].rearrange("p (t c) -> p c t", c=CH), AX_X,
                                        ALU.add).then_inc(s_lsm, 1)

            def step(b, l0, more):
                for j in range(1, TILES):
                    logits(b, j)
                    rows = ROWS_AT.get(j, []) if l0 else []
                    if j >= 2:
                        total2(b, j - 2)
                    if rows:
                        row(b + 1, rows[0])
                    if j == TILES - 1:
                        flags(b)
                    if j >= 2:
                        total3(b, j - 2)
                    masked(b, j - 1)
                    for r in rows[1:]:
                        row(b + 1, r)
                    if l0 and j == J_X1:
                        dve.wait_ge(s_x1, b + 2)
                        mean(2 * (b + 1) + 1, x1_next)
                    if l0 and j == J_CENTER:
                        variance(2 * (b + 1) + 1)
                    if more and j == J_NEXT:
                        dve.wait_ge(s_x, 16 * (b + 3))
                        mean(2 * (b + 2), x_in)
                    if l0 and j == TILES - 1:
                        leaky(b + 1)
                    total1(b, j - 1)
                total2(b, TILES - 2)
                total3(b, TILES - 2)
                masked(b, TILES - 1)
                total1(b, TILES - 1)
                total2(b, TILES - 1)
                total3(b, TILES - 1)
                if l0:
                    logits(b + 1, 0)
                lone_sums(b)
                if more:
                    variance(2 * (b + 2))

            nc.vector.memset(uniform[:, :], 1.0 / NODES).then_inc(s_const, 1)
            dve.wait_ge(s_x, 16)
            mean(0, x_in)
            row(0, 0)
            variance(0)
            for r in range(1, TILES + 1):
                row(0, r)
            dve.wait_ge(s_x1, 1)
            mean(1, x1_next)
            variance(1)
            dve.wait_ge(s_x, 32)
            mean(2, x_in)
            leaky(0)
            logits(0, 0)
            variance(2)
            with dve.Fori(0, BATCH - 2) as b:
                step(b, True, True)
            step(BATCH - 2, True, False)
            step(BATCH - 1, False, False)

        @block.scalar
        def _(act):
            def left_row(b, r):
                base = work_base(b) + TURN_AT[r]
                for g in range(TURNS[r]):
                    w = (min(4 * g + 4, r) - 4 * g) * P
                    at = LEFT_AT[r % 2] + g * CHUNK
                    k = TURN_AT[r] + g
                    act.wait_ge(s_filled, base + g + 1)
                    nc.scalar.activation(left[:, at:at + w], bank(k)[:, 0:w], ACT.Identity,
                                         accum_out=deg_part[:, 6 * r + 2 + g:6 * r + 3 + g]).then_inc(s_drained, 1)

            def scale_row(b, r):
                if r == 0:
                    act.wait_ge(s_norm, 2 * b + 1)
                act.wait_ge(s_deg, TILES * b + r + 1)
                if r >= 2:
                    act.wait_ge(s_mm0, TILES * b + r - 1)
                nc.scalar.activation(scaled[r % 2][:, :], x_norm[:, r * CH:(r + 1) * CH], ACT.Relu,
                                     scale=deg_inv[:, r:r + 1]).then_inc(s_scaled, 1)

            def agg_out(b):
                act.wait_ge(s_mm0, TILES * (b + 1))
                nc.scalar.activation(left[:, AGG_T:AGG_T + ROW], acc0[:, :], ACT.Copy).then_inc(s_agg, 1)

            def to_nodes(dest, n_static, m):
                d = dest[:, m * HALF:(m + 1) * HALF].rearrange("p (h k c) -> p k h c", h=2, c=CH)
                s = bank(n_static).rearrange("p (k h c) -> p k h c", k=4, c=CH)
                return d, s

            def agg_back(b):
                for m in range(2):
                    act.wait_ge(s_filled, work_base(b) + W_AGG + m + 1)
                    d, s = to_nodes(x_norm, W_AGG + m, m)
                    nc.scalar.activation(d, s, ACT.Copy).then_inc(s_drained, 1)

            def square(n):
                act.wait_ge(s_cent, n + 1)
                nc.scalar.activation(left[:, AGG_T:AGG_T + ROW], x_norm[:, :], ACT.Square).then_inc(s_sq, 1)

            def activ_t(b):
                for m in range(2):
                    act.wait_ge(s_filled, work_base(b) + W_XN + m + 1)
                    nc.scalar.activation(left[:, ACTIV_T + m * HALF:ACTIV_T + (m + 1) * HALF], bank(W_XN + m),
                                         ACT.Relu).then_inc(s_drained, 1)

            def hidden_t_out(b):
                for m in range(2):
                    act.wait_ge(s_filled, work_base(b) + W_HID + m + 1)
                    nc.scalar.activation(left[:, LEAKY_T + m * HALF:LEAKY_T + (m + 1) * HALF], bank(W_HID + m),
                                         ACT.Copy).then_inc(s_drained, 1)

            def src_out(b):
                if not (isinstance(b, int) and b == 0):
                    act.wait_ge(s_t, TILES * b)
                row = src_row[:, :].rearrange("p (q two n) -> p two q n", two=2, n=P)
                for k in range(4):
                    act.wait_ge(s_filled, work_base(b) + W_SRC + k + 1)
                    nc.scalar.activation(row[:, k // 2, 4 * (k % 2):4 * (k % 2) + 4, :],
                                         bank(W_SRC + k).rearrange("p (q n) -> p q n", n=P), ACT.Copy,
                                         scale=0.25).then_inc(s_drained, 1)

            def dst_out(b):
                if not (isinstance(b, int) and b == 0):
                    act.wait_ge(s_p, CHUNKS * TILES * b)
                for m in range(2):
                    act.wait_ge(s_filled, work_base(b) + W_DST + m + 1)
                    nc.scalar.activation(dst[:, m * 8:(m + 1) * 8], bank(W_DST + m)[:, 0:8], ACT.Copy,
                                         scale=0.2).then_inc(s_drained, 1)

            def exponentials(b, j, chunks):
                act.wait_ge(s_t, TILES * b + j + 1)
                for q in chunks:
                    if j > 0 or q >= 2:
                        act.wait_ge(s_p, CHUNKS * (TILES * b + j) + q - 1)
                    nc.scalar.activation(exps[:, (q % 2) * CHUNK:(q % 2 + 1) * CHUNK],
                                         adjt[j % ADJT_SLOTS][:, q * CHUNK:(q + 1) * CHUNK], ACT.Exp,
                                         bias=low[:, j:j + 1], scale=-1.0).then_inc(s_e, 1)

            def weigh(b, j):
                if j == 0:
                    act.wait_ge(s_drained, work_base(b) + W_NAT + 2)
                act.wait_ge(s_z, TILES * b + j + 1)
                if j >= 2:
                    act.wait_ge(s_mm1, TILES * b + j - 1)
                nc.scalar.activation(weighed[j % 2][:, :], hidden[:, j * CH:(j + 1) * CH], ACT.Copy,
                                     scale=total[:, j:j + 1]).then_inc(s_hz, 1)

            def acc1_out(b):
                act.wait_ge(s_acc1, b + 1)
                nc.scalar.activation(left[:, LEAKY_T:LEAKY_T + ROW], acc1[:, :], ACT.Copy).then_inc(s_hpt, 1)

            def hidden_out(b):
                for m in range(2):
                    act.wait_ge(s_filled, work_base(b) + W_NAT + m + 1)
                    nc.scalar.activation(hidden[:, m * HALF:(m + 1) * HALF], bank(W_NAT + m),
                                         ACT.Copy).then_inc(s_drained, 1)

            def relu_out(base, k):
                for m in range(2):
                    act.wait_ge(s_filled, base + k + m + 1)
                    d, s = to_nodes(left[:, AGG_T:AGG_T + ROW], k + m, m)
                    nc.scalar.activation(d, s, ACT.Relu).then_inc(s_drained, 1)

            def move_x1():
                nc.scalar.activation(x1[:, :], x1_next[:, :], ACT.Copy).then_inc(s_x1m, 1)

            def step(b, l0, more):
                for j in range(1, TILES):
                    rows = ROWS_AT.get(j, []) if l0 else []
                    if rows and 1 <= rows[0] < TILES:
                        left_row(b + 1, rows[0])
                    if l0 and j == J_AGG:
                        agg_out(b + 1)
                    if l0 and j == J_CENTER:
                        square(2 * (b + 1) + 1)
                    if l0 and j == TILES - 1:
                        activ_t(b + 1)
                    if j >= 2:
                        weigh(b, j - 2)
                    exponentials(b, j - 1, (2, 3))
                    exponentials(b, j, (0, 1))
                    for n, r in enumerate(rows):
                        if n > 0:
                            left_row(b + 1, r)
                        if r >= 1:
                            scale_row(b + 1, r - 1)
                    if l0 and j == J_AGG:
                        agg_back(b + 1)
                if l0:
                    hidden_t_out(b + 1)
                weigh(b, TILES - 2)
                exponentials(b, TILES - 1, (2, 3))
                if l0:
                    src_out(b + 1)
                    dst_out(b + 1)
                weigh(b, TILES - 1)
                if more:
                    square(2 * (b + 2))
                if l0:
                    exponentials(b + 1, 0, (0, 1))
                if more:
                    act.wait_ge(s_var, 2 * (b + 2) + 1)
                acc1_out(b)
                if l0:
                    act.wait_ge(s_lsm, b + 1)
                    hidden_out(b + 1)
                    relu_out(work_base(b + 1), W_OUT)
                    act.wait_ge(s_out, b + 1)
                    move_x1()
                else:
                    relu_out(work_base(b + 1), 0)

            k = 0
            for r in range(TILES):
                for c in range(r, TILES, 4):
                    w = (min(c + 4, TILES) - c) * P
                    act.wait_ge(s_filled, k + 1)
                    at = GATE_AT[r] + (c - r) * P
                    nc.scalar.activation(gate[:, at:at + w], bank(k)[:, 0:w], ACT.Sigmoid).then_inc(s_drained, 1)
                    k += 1
            square(0)
            for r in range(TILES + 1):
                if 1 <= r < TILES:
                    left_row(0, r)
                if r >= 1:
                    scale_row(0, r - 1)
            agg_out(0)
            agg_back(0)
            square(1)
            activ_t(0)
            hidden_t_out(0)
            src_out(0)
            dst_out(0)
            square(2)
            exponentials(0, 0, (0, 1))
            hidden_out(0)
            act.wait_ge(s_x1, 1)
            move_x1()
            with act.Fori(0, BATCH - 2) as b:
                step(b, True, True)
            step(BATCH - 2, True, False)
            step(BATCH - 1, False, False)

        @block.tensor
        def _(pe):
            def free_bank(n):
                pe.wait_ge(s_drained, n - 1)

            def turn_row(b, r):
                pe.wait_ge(s_k, len(UNITS) * b + UNITS_OF[r - 1][-1] + 1)
                for g in range(TURNS[r]):
                    k = TURN_AT[r] + g
                    free_bank(work_base(b) + k)
                    for c in range(4 * g, min(4 * g + 4, r)):
                        at = K_AT[c] + (r - c) * P
                        t = pe.transpose(bank(k)[:, (c % 4) * P:(c % 4 + 1) * P], k_rows[:, at:at + P], ident)
                    t.then_inc(s_filled, 1)

            def multiply_row(b, r):
                pe.wait_ge(s_scaled, TILES * b + r + 1)
                if r == 0 and not (isinstance(b, int) and b == 0):
                    pe.wait_ge(s_agg, b)
                for q in range(CHUNKS):
                    lo, hi = q * CHUNK, (q + 1) * CHUNK
                    mid = min(max(r * P, lo), hi)
                    acc = chunk_of(acc0, q)
                    lw = scaled[r % 2][:, :]
                    parts = []
                    if lo < mid:
                        at = LEFT_AT[r % 2]
                        parts.append((lo, mid, left[:, at + lo:at + mid]))
                    if mid < hi:
                        at = K_AT[r] - r * P
                        parts.append((mid, hi, k_rows[:, at + mid:at + hi]))
                    for n, (a, z, rhs) in enumerate(parts):
                        m = pe.matmul(acc[:, a - lo:z - lo], lw, rhs, start=(r == 0),
                                      stop=(r == TILES - 1 and n == len(parts) - 1))
                m.then_inc(s_mm0, 1)

            def turn_back(base, k0, region):
                for m in range(2):
                    free_bank(base + k0 + m)
                    for k in range(4):
                        at = region + (4 * m + k) * P
                        t = pe.transpose(bank(k0 + m)[:, k * P:(k + 1) * P], left[:, at:at + P], ident)
                    t.then_inc(s_filled, 1)

            def turn_norm(b):
                pe.wait_ge(s_norm, 2 * b + 2)
                for m in range(2):
                    free_bank(work_base(b) + W_XN + m)
                    for k in range(4):
                        q = 4 * m + k
                        t = pe.transpose(bank(W_XN + m)[:, k * P:(k + 1) * P], x_norm[:, q * P:(q + 1) * P], ident)
                    t.then_inc(s_filled, 1)

            def hidden_t(b):
                pe.wait_ge(s_drained, work_base(b) + W_XN + 2)
                for m in range(2):
                    free_bank(work_base(b) + W_HID + m)
                    pe.matmul(bank(W_HID + m), w_pair, left[:, ACTIV_T + m * HALF:ACTIV_T + (m + 1) * HALF],
                              start=True, stop=True).then_inc(s_filled, 1)

            def src_and_dst(b):
                pe.wait_ge(s_leaky, b + 1)
                for k in range(4):
                    free_bank(work_base(b) + W_SRC + k)
                    at = LEAKY_T + (k % 2) * HALF
                    pe.matmul(bank(W_SRC + k), cst[:, C_SRC + (k // 2) * P:C_SRC + (k // 2 + 1) * P],
                              left[:, at:at + HALF], start=True, stop=True).then_inc(s_filled, 1)
                for m in range(2):
                    free_bank(work_base(b) + W_DST + m)
                    for k in range(4):
                        at = LEAKY_T + (4 * m + k) * P
                        t = pe.matmul(bank(W_DST + m)[:, 2 * k:2 * k + 2], left[:, at:at + P],
                                      cst[:, C_DST:C_DST + 2], start=True, stop=True)
                    t.then_inc(s_filled, 1)

            def hidden_nodes(b):
                for m in range(2):
                    free_bank(work_base(b) + W_NAT + m)
                    for k in range(4):
                        at = ACTIV_T + (4 * m + k) * P
                        t = pe.matmul(bank(W_NAT + m)[:, k * P:(k + 1) * P], left[:, at:at + P], w_pair,
                                      start=True, stop=True)
                    t.then_inc(s_filled, 1)

            def gather_row(b, j):
                pe.wait_ge(s_hz, TILES * b + j + 1)
                for q in range(CHUNKS):
                    m = pe.matmul(chunk_of(acc1, q), weighed[j % 2][:, :],
                                  adjt[j % ADJT_SLOTS][:, q * CHUNK:(q + 1) * CHUNK], start=(j == 0), stop=False)
                m.then_inc(s_mm1, 1)

            def gather_lone(b):
                pe.wait_ge(s_lsm, b + 1)
                for q in range(CHUNKS):
                    m = pe.matmul(chunk_of(acc1, q), lone_sum[:, :], uniform[:, 0:1].to_broadcast([P, CHUNK]),
                                  start=False, stop=True)
                m.then_inc(s_acc1, 1)

            def step(b, l0, more):
                for j in range(1, TILES):
                    rows = ROWS_AT.get(j, []) if l0 else []
                    if rows and 1 <= rows[0] < TILES:
                        turn_row(b + 1, rows[0])
                    if l0 and j == TILES - 1:
                        turn_norm(b + 1)
                    if j >= 2:
                        gather_row(b, j - 2)
                    for n, r in enumerate(rows):
                        if n > 0:
                            turn_row(b + 1, r)
                        if r >= 1:
                            multiply_row(b + 1, r - 1)
                    if l0 and j == J_AGG:
                        pe.wait_ge(s_agg, b + 2)
                        turn_back(work_base(b + 1), W_AGG, AGG_T)
                    if l0 and j == TILES - 1:
                        hidden_t(b + 1)
                if l0:
                    src_and_dst(b + 1)
                gather_row(b, TILES - 2)
                gather_row(b, TILES - 1)
                gather_lone(b)
                if l0:
                    hidden_nodes(b + 1)
                pe.wait_ge(s_hpt, b + 1)
                turn_back(work_base(b + 1), W_OUT if l0 else 0, LEAKY_T)

            pe.wait_ge(s_u, 16)
            k = 0
            for r in range(TILES):
                for c in range(r, TILES, 4):
                    w = (min(c + 4, TILES) - c) * P
                    if k >= 2:
                        free_bank(k)
                    pe.matmul(bank(k)[:, 0:w], u_sb[:, r * P:(r + 1) * P], u_sb[:, c * P:c * P + w],
                              start=True, stop=True).then_inc(s_filled, 1)
                    k += 1
            pe.wait_ge(s_cst, 16)
            pe.wait_ge(s_const, 2)
            for r in range(TILES + 1):
                if 1 <= r < TILES:
                    turn_row(0, r)
                if r >= 1:
                    multiply_row(0, r - 1)
            pe.wait_ge(s_agg, 1)
            turn_back(work_base(0), W_AGG, AGG_T)
            turn_norm(0)
            hidden_t(0)
            src_and_dst(0)
            hidden_nodes(0)
            with pe.Fori(0, BATCH - 2) as b:
                step(b, True, True)
            step(BATCH - 2, True, False)
            step(BATCH - 1, False, False)


def kernel(x, adj, L0_gnn_U, L0_gnn_w_scale, L1_gnn_W, L1_gnn_a):
    import concourse.bacc as bacc
    from concourse.bass_utils import run_bass_kernel_spmd

    x, adj, u, w_scale, w, a = (np.asarray(v) for v in (x, adj, L0_gnn_U, L0_gnn_w_scale, L1_gnn_W, L1_gnn_a))
    rows = np.ascontiguousarray(x.reshape(BATCH, TILES, P, CH).transpose(0, 2, 1, 3).reshape(BATCH, P, ROW))
    adj_t = np.ascontiguousarray(adj.transpose(0, 2, 1)).reshape(BATCH, TILES, P, NODES)
    tiled = adj.reshape(BATCH, TILES, P, NODES)
    pairs = np.empty((BATCH, P, PAIR_ROW), np.float32)
    for n, (r, c0, c1) in enumerate(UNITS):
        mid = (PAIR_AT[n] + PAIR_AT[n + 1]) // 2
        pairs[:, :, PAIR_AT[n]:mid] = tiled[:, r, :, c0 * P:c1 * P]
        pairs[:, :, mid:PAIR_AT[n + 1]] = adj_t[:, r, :, c0 * P:c1 * P]
    consts = np.zeros((P, C_COLS), np.float32)
    consts[:, C_ID:C_ID + P] = np.eye(P, dtype=np.float32)
    for half in range(2):
        at = slice(half * CH, (half + 1) * CH)
        consts[at, C_W + half * CH:C_W + (half + 1) * CH] = w
        consts[at, C_SRC + half * P:C_SRC + (half + 1) * P] = a[:CH]
        consts[at, C_DST + half] = a[CH:, 0]
    consts[:, C_SCALE] = w_scale
    arrays = {"x_rows": rows, "adj_pairs": pairs, "adj_t": adj_t, "u_t": np.ascontiguousarray(u.T), "consts": consts}
    nc = bacc.Bacc("TRN2", target_bir_lowering=False, num_devices=1, dynamic_dma_scratch_size=1024)
    aps = [nc.dram_tensor(name, v.shape, F32, kind="ExternalInput").ap() for name, v in arrays.items()]
    out = nc.dram_tensor("out_rows", (BATCH, P, ROW), F32, kind="ExternalOutput").ap()
    gnn_program(nc, *aps, out)
    got = run_bass_kernel_spmd(nc, [arrays], core_ids=[0]).results[0]["out_rows"]
    return np.ascontiguousarray(got.reshape(BATCH, P, TILES, CH).transpose(0, 2, 1, 3).reshape(BATCH, NODES, CH))
```

```python
from contextlib import ExitStack

import numpy as np
import concourse.bass as bass
from concourse import mybir

F32 = mybir.dt.float32
ALU = mybir.AluOpType
ACT = mybir.ActivationFunctionType
AX_X = mybir.AxisListType.X

P = 128
BATCH, NODES, CH, RANK = 8, 2048, 64, 16
TILES = NODES // P
ROW = TILES * CH
CHUNK = 512
CHUNKS = NODES // CHUNK
HALF = ROW // 2

UNIT = 8
UNITS = [(r, c, min(c + UNIT, TILES)) for r in range(TILES) for c in range(r, TILES, UNIT)]
UNITS_OF = [[n for n, (row, _, _) in enumerate(UNITS) if row == r] for r in range(TILES)]
PAIR_SLOTS = 3
ADJT_SLOTS = 4
assert len(UNITS) % PAIR_SLOTS == 0 and TILES % ADJT_SLOTS == 0
PAIR_AT = np.cumsum([0] + [2 * (c1 - c0) * P for _, c0, c1 in UNITS]).tolist()
PAIR_ROW = PAIR_AT[-1]

GATE_AT = np.cumsum([0] + [(TILES - r) * P for r in range(TILES)]).tolist()
K_AT = GATE_AT[:8] * 2
K_ROW = GATE_AT[8]
LEFTS = 3
LEFT_MAX = [max(r for r in range(TILES) if r % LEFTS == n) for n in range(LEFTS)]
LEFT_AT = np.cumsum([0] + [blocks * P for blocks in LEFT_MAX]).tolist()
LEFT_ROW = LEFT_AT[-1]
AGG_T, ACTIV_T, LEAKY_T, X1_NEW, X1_OLD = 0, ROW, 2 * ROW, 3 * ROW, 4 * ROW
assert X1_OLD + ROW <= LEFT_ROW

TURNS = [-(-r // 4) for r in range(TILES)]
FIRST, REST = slice(0, 2), slice(2, None)
TURN_AT = np.cumsum([0] + TURNS).tolist()
W_AGG = TURN_AT[-1]
W_XN = W_AGG + 2
W_HID = W_XN + 2
W_SRC = W_HID + 2
W_DST = W_SRC + 4
W_NAT = W_DST + 2
W_OUT = W_NAT + 2
W_STEP = W_STEP_END = W_OUT + 2
GATE_TURNS_BY = np.cumsum([-(-(TILES - r) // 4) for r in range(TILES)]).tolist()
W_GATES = sum(-(-(TILES - r) // 4) for r in range(TILES))
assert W_GATES % 2 == 0 and W_STEP % 2 == 0

ROWS_AT = {1: [1, 2], 2: [3, 4], 3: [5, 6], 4: [7, 8], 5: [9, 10], 6: [11, 12], 7: [13, 14],
           8: [15, 16], 9: [17]}
K_IN = {r: [r] if r >= UNIT else [r + 1] if r + 1 < UNIT else [] for r in range(TILES)}
SUM_IN = {r: [r + 1] if r + 1 in range(UNIT, TILES) else [] for r in range(TILES)}
SUMS_AHEAD_AT = {9: [0], 10: [1], 11: [2], 12: [3], 13: [4], 14: [5]}
SUMS_AHEAD_END = [6]
SUMS_LATE_AT = {1: [7]}
J_AGG, J_X1, J_CENTER, J_NORM, J_TURN, J_NEXT = 10, 11, 12, 13, 14, 14

C_ID, C_W, C_SRC, C_DST, C_SCALE = 0, P, 2 * P, 4 * P, 4 * P + 2
C_COLS = C_SCALE + 1


def work_base(b):
    return W_GATES if isinstance(b, int) and b == 0 else W_GATES + W_OUT + W_STEP * (b - 1)


def gnn_program(nc, x, pairs, adj_t, u_t, consts, x1_store, out):
    with ExitStack() as ctx:
        def sb(name, cols, parts=P):
            return ctx.enter_context(nc.sbuf_tensor(name, [parts, cols], F32))

        def sem(name):
            return ctx.enter_context(nc.semaphore(name))

        gate = sb("gate", GATE_AT[-1])
        k_rows = sb("k_rows", K_ROW)
        left = sb("left", LEFT_ROW)
        pair = [sb(f"pair{i}", 2 * UNIT * P) for i in range(PAIR_SLOTS)]
        adjt = [sb(f"adjt{i}", NODES) for i in range(ADJT_SLOTS)]
        src_row = sb("src_row", NODES)
        x_in = sb("x_in", ROW)
        x_norm = sb("x_norm", ROW)
        hidden = sb("hidden", ROW)
        cst = sb("cst", C_COLS)
        scaled = [sb(f"scaled{i}", CH) for i in range(2)]
        weighed = [sb(f"weighed{i}", CH) for i in range(2)]
        deg_part = sb("deg_part", TILES * 6)
        deg = sb("deg", TILES)
        deg_inv = sb("deg_inv", TILES)
        deg_out = sb("deg_out", TILES)
        minus_half = sb("minus_half", TILES)
        ln_mean = sb("ln_mean", TILES)
        ln_var = sb("ln_var", TILES)
        low = sb("low", TILES)
        dst = sb("dst", TILES)
        flag = sb("flag", TILES)
        part_sum = sb("part_sum", TILES * 4)
        total = sb("total", TILES)
        lone_sum = sb("lone_sum", CH)
        uniform = sb("uniform", 1)
        u_sb = src_row[0:RANK, :]

        acc0 = ctx.enter_context(nc.psum_tensor("acc0", [P, 2 * CHUNK], F32))
        acc1 = ctx.enter_context(nc.psum_tensor("acc1", [P, 2 * CHUNK], F32))
        exps = ctx.enter_context(nc.psum_tensor("exps", [P, 2 * CHUNK], F32))
        work = ctx.enter_context(nc.psum_tensor("work", [P, 2 * CHUNK], F32))

        s_cst = sem("consts_loaded")
        s_u = sem("u_loaded")
        s_pair = [sem(f"pair_loaded{i}") for i in range(PAIR_SLOTS)]
        s_adjt = [sem(f"adjt_loaded{i}") for i in range(ADJT_SLOTS)]
        s_x = sem("x_loaded")
        s_stored = sem("x1_and_out_stored")
        s_const = sem("small_consts_set")
        s_filled = sem("work_filled")
        s_drained = sem("work_drained")
        s_sum = sem("pairs_summed")
        s_k = sem("k_units_made")
        s_degp = sem("degrees_summed")
        s_degc = sem("degrees_clamped")
        s_deg = sem("degrees_inverted")
        s_scaled = sem("scaled_rows_made")
        s_mm0 = sem("layer0_rows_multiplied")
        s_agg = sem("agg_copied")
        s_dw = sem("deg_out_made")
        s_aggs = sem("agg_scaled")
        s_x1 = sem("x1_made")
        s_x1ld = sem("x1_loaded")
        s_lsum = sem("ln_summed")
        s_mean = sem("ln_mean_made")
        s_cent = sem("ln_centered")
        s_sq = sem("ln_squared")
        s_vsum = sem("ln_squares_summed")
        s_var = sem("ln_var_made")
        s_rstd = sem("ln_rstd_made")
        s_norm = sem("ln_normed")
        s_leaky = sem("leaky_made")
        s_begun = sem("logits_begun")
        s_t = sem("logits_made")
        s_e = sem("exp_chunks_made")
        s_p = sem("masked_chunks_made")
        s_z1 = sem("totals_summed")
        s_z2 = sem("totals_clamped")
        s_z = sem("totals_inverted")
        s_hz = sem("weighed_rows_made")
        s_mm1 = sem("layer1_rows_multiplied")
        s_flag = sem("lone_flags_made")
        s_lone = sem("lone_hidden_made")
        s_lsm = sem("lone_sum_made")
        s_acc1 = sem("acc1_complete")
        s_hpt = sem("acc1_copied")
        s_out = sem("out_made")

        ident = cst[:, C_ID:C_ID + P]
        w_pair = cst[:, C_W:C_W + P]

        def bank(n):
            return work[:, (n % 2) * CHUNK:(n % 2 + 1) * CHUNK]

        def tch(ap):
            return ap.rearrange("p (t c) -> p t c", c=CH)

        def per_tile(col):
            return col[:, :].unsqueeze(2).to_broadcast([P, TILES, CH])

        def chunk_of(acc, q):
            return acc[CH * (q % 2):CH * (q % 2) + CH, (q // 2) * CHUNK:(q // 2 + 1) * CHUNK]

        x1_next = left[:, X1_NEW:X1_NEW + ROW]
        x1 = left[:, X1_OLD:X1_OLD + ROW]

        block = ctx.enter_context(nc.Block())

        @block.sync
        def _(sp):
            def load_pair(b, n):
                sp.dma_start(pair[n % PAIR_SLOTS][:, 0:PAIR_AT[n + 1] - PAIR_AT[n]],
                             pairs[b, :, PAIR_AT[n]:PAIR_AT[n + 1]]).then_inc(s_pair[n % PAIR_SLOTS], 16)

            def load_pairs_behind(b, rows, last):
                for n in [n for r in rows for n in UNITS_OF[r]]:
                    if n + PAIR_SLOTS < len(UNITS):
                        sp.wait_ge(s_sum, len(UNITS) * b + n + 1)
                        load_pair(b, n + PAIR_SLOTS)
                    elif not last:
                        sp.wait_ge(s_sum, len(UNITS) * b + n + 1)
                        load_pair(b + 1, n + PAIR_SLOTS - len(UNITS))

            def load_adjt(b, j):
                sp.dma_start(adjt[j % ADJT_SLOTS][:, :], adj_t[b, j, :, :]).then_inc(s_adjt[j % ADJT_SLOTS], 16)

            def load_adjt_behind(b, j, last):
                nxt = j + ADJT_SLOTS
                if nxt < TILES:
                    sp.wait_ge(s_mm1, TILES * b + j + 1)
                    load_adjt(b, nxt)
                elif not last:
                    sp.wait_ge(s_mm1, TILES * b + j + 1)
                    load_adjt(b + 1, nxt - TILES)

            def load_x(b):
                sp.dma_start(x_in[:, :], x[b, :, :]).then_inc(s_x, 16)

            def store_x1(b):
                sp.dma_start(x1_store[b, :, :], x1_next).then_inc(s_stored, 16)

            def step(b, l0, more):
                for j in range(1, TILES):
                    if l0:
                        load_pairs_behind(b + 1, SUMS_LATE_AT.get(j, []), not more)
                        load_pairs_behind(b + 1, [q for r in ROWS_AT.get(j, []) for q in SUM_IN.get(r, [])], not more)
                    if j >= 2:
                        load_adjt_behind(b, j - 2, not l0)
                    if more:
                        load_pairs_behind(b + 2, SUMS_AHEAD_AT.get(j, []), False)
                    if j == J_CENTER:
                        if l0:
                            sp.wait_ge(s_x1, b + 2)
                        if more:
                            load_x(b + 2)
                        if l0:
                            store_x1(b + 1)
                    if j == J_CENTER + 1:
                        sp.wait_ge(s_stored, 16 * (2 * b + (2 if l0 else 1)))
                        sp.dma_start(x1, x1_store[b, :, :]).then_inc(s_x1ld, 16)
                load_adjt_behind(b, TILES - 2, not l0)
                if more:
                    load_pairs_behind(b + 2, SUMS_AHEAD_END, False)
                sp.wait_ge(s_out, b + 1)
                sp.dma_start(out[b, :, :], left[:, AGG_T:AGG_T + ROW]).then_inc(s_stored, 16)
                sp.wait_ge(s_stored, 16 * (2 * b + (3 if l0 else 2)))
                if l0:
                    load_adjt(b + 1, ADJT_SLOTS - 1)

            sp.dma_start(u_sb, u_t[:, :]).then_inc(s_u, 16)
            load_pair(0, 0)
            sp.dma_start(cst[:, :], consts[:, :]).then_inc(s_cst, 16)
            load_x(0)
            for n in range(1, PAIR_SLOTS):
                load_pair(0, n)
            for j in range(ADJT_SLOTS):
                load_adjt(0, j)
            load_pairs_behind(0, range(TILES), False)
            sp.wait_ge(s_x1, 1)
            load_x(1)
            store_x1(0)
            load_pairs_behind(1, range(UNIT - 1), False)
            with sp.Fori(0, BATCH - 2) as b:
                step(b, True, True)
            step(BATCH - 2, True, False)
            step(BATCH - 1, False, False)

        @block.gpsimd
        def _(pool):
            def sum_row(b, r):
                if r >= UNIT:
                    if r == UNIT:
                        pool.wait_ge(s_filled, work_base(b) + TURN_AT[UNIT])
                    pool.wait_ge(s_mm0, TILES * b + r - UNIT + 1)
                elif r == 0 and not (isinstance(b, int) and b == 0):
                    pool.wait_ge(s_filled, work_base(b - 1) + TURN_AT[TILES])
                    pool.wait_ge(s_mm0, TILES * b - 3)
                elif r == 5 and not (isinstance(b, int) and b == 0):
                    pool.wait_ge(s_mm0, TILES * b)
                for n in UNITS_OF[r]:
                    pool.wait_ge(s_pair[n % PAIR_SLOTS], 16 * (len(UNITS) // PAIR_SLOTS * b + n // PAIR_SLOTS + 1))
                    w = (PAIR_AT[n + 1] - PAIR_AT[n]) // 2
                    at = K_AT[r] + (UNITS[n][1] - r) * P
                    p = pair[n % PAIR_SLOTS]
                    nc.gpsimd.tensor_tensor(k_rows[:, at:at + w], p[:, 0:w], p[:, w:2 * w], ALU.add).then_inc(s_sum, 1)

            def invert_degree(b, r):
                pool.wait_ge(s_degc, TILES * b + r + 1)
                nc.gpsimd.tensor_tensor(deg_inv[:, r:r + 1], deg[:, r:r + 1], minus_half[:, r:r + 1],
                                        ALU.pow).then_inc(s_deg, 1)

            def row(b, r):
                if r >= 2:
                    invert_degree(b, r - 2)
                for q in SUM_IN.get(r, []):
                    sum_row(b, q)

            def add_layer0(b):
                pool.wait_ge(s_deg, TILES * (b + 1))
                nc.gpsimd.tensor_tensor(deg_out[:, :], deg_inv[:, :],
                                        cst[:, C_SCALE:C_SCALE + 1].to_broadcast([P, TILES]), ALU.mult).then_inc(s_dw, 1)
                pool.wait_ge(s_dw, b + 1)
                pool.wait_ge(s_drained, work_base(b) + W_AGG + 2)
                nc.gpsimd.tensor_tensor(tch(x_norm[:, :]), tch(x_norm[:, :]), per_tile(deg_out),
                                        ALU.mult).then_inc(s_aggs, 1)
                pool.wait_ge(s_aggs, b + 1)
                nc.gpsimd.tensor_tensor(x1_next, x_norm[:, :], x_in[:, :], ALU.add).then_inc(s_x1, 1)

            def center(n, source):
                pool.wait_ge(s_mean, n + 1)
                nc.gpsimd.tensor_tensor(tch(x_norm[:, :]), tch(source), per_tile(ln_mean),
                                        ALU.subtract).then_inc(s_cent, 1)

            def normalize(n):
                pool.wait_ge(s_var, n + 1)
                nc.gpsimd.tensor_tensor(ln_var[:, :], ln_var[:, :], minus_half[:, :], ALU.pow).then_inc(s_rstd, 1)
                pool.wait_ge(s_rstd, n + 1)
                nc.gpsimd.tensor_tensor(tch(x_norm[:, :]), tch(x_norm[:, :]), per_tile(ln_var),
                                        ALU.mult).then_inc(s_norm, 1)

            def lone(b):
                pool.wait_ge(s_flag, b + 1)
                pool.wait_ge(s_hz, TILES * (b + 1))
                nc.gpsimd.tensor_tensor(tch(hidden[:, :]), tch(hidden[:, :]), per_tile(flag),
                                        ALU.mult).then_inc(s_lone, 1)

            def add_layer1(b, relu_at):
                pool.wait_ge(s_drained, relu_at)
                pool.wait_ge(s_x1ld, 16 * (b + 1))
                res = left[:, AGG_T:AGG_T + ROW]
                nc.gpsimd.tensor_tensor(res, res, x1, ALU.add).then_inc(s_out, 1)

            def step(b, l0, more):
                for j in range(1, TILES):
                    if l0:
                        for r in SUMS_LATE_AT.get(j, []):
                            sum_row(b + 1, r)
                        for r in ROWS_AT.get(j, []):
                            row(b + 1, r)
                        if j == J_X1:
                            add_layer0(b + 1)
                        if j == J_CENTER:
                            center(2 * (b + 1) + 1, x1_next)
                        if j == J_NORM:
                            normalize(2 * (b + 1) + 1)
                    if more:
                        for r in SUMS_AHEAD_AT.get(j, []):
                            sum_row(b + 2, r)
                if more:
                    pool.wait_ge(s_filled, work_base(b + 1) + W_XN + 2)
                    center(2 * (b + 2), x_in[:, :])
                lone(b)
                if more:
                    for r in SUMS_AHEAD_END:
                        sum_row(b + 2, r)
                if more:
                    normalize(2 * (b + 2))
                add_layer1(b, work_base(b + 1) + (W_STEP_END if l0 else 2))

            nc.gpsimd.memset(minus_half[:, :], -0.5).then_inc(s_const, 1)
            pool.wait_ge(s_const, 1)
            center(0, x_in[:, :])
            for r in range(UNIT):
                sum_row(0, r)
                if r == 0:
                    normalize(0)
            for r in range(2, TILES + 2):
                row(0, r)
            pool.wait_ge(s_cst, 16)
            sum_row(1, 0)
            add_layer0(0)
            sum_row(1, 1)
            center(1, x1_next)
            normalize(1)
            pool.wait_ge(s_filled, work_base(0) + W_XN + 2)
            center(2, x_in[:, :])
            normalize(2)
            for r in range(2, UNIT - 1):
                sum_row(1, r)
            with pool.Fori(0, BATCH - 2) as b:
                step(b, True, True)
            step(BATCH - 2, True, False)
            step(BATCH - 1, False, False)

        @block.vector
        def _(dve):
            def k_unit(b, n):
                r, c0, c1 = UNITS[n]
                dve.wait_ge(s_sum, len(UNITS) * b + n + 1)
                if isinstance(b, int) and b == 0:
                    dve.wait_ge(s_drained, GATE_TURNS_BY[r])
                at, w = (c0 - r) * P, (c1 - c0) * P
                col = 6 * r + (1 if r >= UNIT or c0 > r else 0)
                k = k_rows[:, K_AT[r] + at:K_AT[r] + at + w]
                nc.vector.tensor_tensor_reduce(k, k,
                                               gate[:, GATE_AT[r] + at:GATE_AT[r] + at + w],
                                               0.5, 0.0, ALU.mult, ALU.add,
                                               deg_part[:, col:col + 1]).then_inc(s_k, 1)

            def degree(b, r):
                if r >= 1:
                    dve.wait_ge(s_drained, work_base(b) + TURN_AT[r] + TURNS[r])
                dve.wait_ge(s_k, len(UNITS) * b + UNITS_OF[r][-1] + 1)
                first = 6 * r + (1 if r >= UNIT else 0)
                nc.vector.tensor_reduce(deg[:, r:r + 1], deg_part[:, first:6 * r + 2 + TURNS[r]], AX_X,
                                        ALU.add).then_inc(s_degp, 1)
                dve.wait_ge(s_degp, TILES * b + r + 1)
                nc.vector.tensor_scalar(deg[:, r:r + 1], deg[:, r:r + 1], 1e-12, None, ALU.max).then_inc(s_degc, 1)

            def make_k(b, rows):
                for r in rows:
                    for n in UNITS_OF[r]:
                        k_unit(b, n)

            def mean(n, source):
                nc.vector.tensor_reduce(ln_mean[:, :], tch(source), AX_X, ALU.add).then_inc(s_lsum, 1)
                dve.wait_ge(s_lsum, n + 1)
                nc.vector.tensor_scalar(ln_mean[:, :], ln_mean[:, :], 1.0 / CH, None, ALU.mult).then_inc(s_mean, 1)

            def variance(n):
                dve.wait_ge(s_sq, n + 1)
                nc.vector.tensor_reduce(ln_var[:, :], tch(left[:, AGG_T:AGG_T + ROW]), AX_X, ALU.add).then_inc(s_vsum, 1)
                dve.wait_ge(s_vsum, n + 1)
                nc.vector.tensor_scalar(ln_var[:, :], ln_var[:, :], 1.0 / CH, 1e-5, ALU.mult, ALU.add).then_inc(s_var, 1)

            def logits(b, j):
                dve.wait_ge(s_adjt[j % ADJT_SLOTS], 16 * (TILES // ADJT_SLOTS * b + j // ADJT_SLOTS + 1))
                if j == 0:
                    dve.wait_ge(s_drained, work_base(b) + W_SRC + 4)
                dve.sem_inc(s_begun, 1)
                a = adjt[j % ADJT_SLOTS][:, :]
                nc.vector.tensor_tensor_reduce(a, a, src_row[:, :], -0.8, 3.0e38, ALU.add, ALU.min,
                                               low[:, j:j + 1]).then_inc(s_t, 1)

            def masked(b, j, chunks):
                if j == 0 and 0 in chunks:
                    dve.wait_ge(s_drained, work_base(b) + W_DST + 2)
                for q in chunks:
                    dve.wait_ge(s_e, CHUNKS * (TILES * b + j) + q + 1)
                    a = adjt[j % ADJT_SLOTS][:, q * CHUNK:(q + 1) * CHUNK]
                    nc.vector.scalar_tensor_tensor(a, a, dst[:, j:j + 1], exps[:, (q % 2) * CHUNK:(q % 2 + 1) * CHUNK],
                                                   ALU.is_lt, ALU.mult,
                                                   part_sum[:, 4 * j + q:4 * j + q + 1]).then_inc(s_p, 1)

            def total1(b, j):
                dve.wait_ge(s_p, CHUNKS * (TILES * b + j + 1))
                nc.vector.tensor_reduce(total[:, j:j + 1], part_sum[:, 4 * j:4 * j + 4], AX_X, ALU.add).then_inc(s_z1, 1)

            def total2(b, j):
                dve.wait_ge(s_z1, TILES * b + j + 1)
                nc.vector.tensor_scalar(total[:, j:j + 1], total[:, j:j + 1], 0.5, None, ALU.max).then_inc(s_z2, 1)

            def total3(b, j):
                dve.wait_ge(s_z2, TILES * b + j + 1)
                nc.vector.reciprocal(total[:, j:j + 1], total[:, j:j + 1]).then_inc(s_z, 1)

            def leaky(b):
                dve.wait_ge(s_drained, work_base(b) + W_HID + 2)
                h = left[:, LEAKY_T:LEAKY_T + ROW]
                nc.vector.scalar_tensor_tensor(h, h, 0.2, h, ALU.mult, ALU.max).then_inc(s_leaky, 1)

            def flags(b):
                dve.wait_ge(s_t, TILES * (b + 1))
                nc.vector.tensor_tensor(flag[:, :], low[:, :], dst[:, :], ALU.is_ge).then_inc(s_flag, 1)

            def lone_sums(b):
                dve.wait_ge(s_lone, b + 1)
                nc.vector.tensor_reduce(lone_sum[:, :], hidden[:, :].rearrange("p (t c) -> p c t", c=CH), AX_X,
                                        ALU.add).then_inc(s_lsm, 1)

            def step(b, l0, more):
                for j in range(1, TILES):
                    rows = ROWS_AT.get(j, []) if l0 else []
                    ended = [r - 2 for r in rows]
                    if j >= 2:
                        total2(b, j - 2)
                    if rows and ended[0] >= 0:
                        degree(b + 1, ended[0])
                    if j >= 2:
                        total3(b, j - 2)
                    if l0 and j == TILES - 1:
                        leaky(b + 1)
                    logits(b, j)
                    if rows[1:] and ended[1] >= 0:
                        degree(b + 1, ended[1])
                    masked(b, j - 1, (0, 1))
                    if rows:
                        make_k(b + 1, K_IN.get(rows[0], []))
                    if j == TILES - 1:
                        flags(b)
                    masked(b, j - 1, (2, 3))
                    for r in rows[1:]:
                        make_k(b + 1, K_IN.get(r, []))
                    if l0 and j == J_X1:
                        dve.wait_ge(s_x1, b + 2)
                        mean(2 * (b + 1) + 1, x1_next)
                    if l0 and j == J_CENTER:
                        variance(2 * (b + 1) + 1)
                    if more and j == J_NEXT:
                        dve.wait_ge(s_x, 16 * (b + 3))
                        mean(2 * (b + 2), x_in[:, :])
                    total1(b, j - 1)
                total2(b, TILES - 2)
                total3(b, TILES - 2)
                masked(b, TILES - 1, (0, 1))
                if more:
                    make_k(b + 2, [0])
                masked(b, TILES - 1, (2, 3))
                total1(b, TILES - 1)
                total2(b, TILES - 1)
                total3(b, TILES - 1)
                if l0:
                    logits(b + 1, 0)
                if more:
                    make_k(b + 2, [1])
                lone_sums(b)
                if more:
                    variance(2 * (b + 2))

            nc.vector.memset(uniform[:, :], 1.0 / NODES).then_inc(s_const, 1)
            dve.wait_ge(s_x, 16)
            mean(0, x_in[:, :])
            make_k(0, [0])
            variance(0)
            make_k(0, [1])
            for r in range(1, TILES + 2):
                if r >= 2:
                    degree(0, r - 2)
                make_k(0, K_IN.get(r, []))
            dve.wait_ge(s_x1, 1)
            mean(1, x1_next)
            variance(1)
            dve.wait_ge(s_x, 32)
            mean(2, x_in[:, :])
            leaky(0)
            make_k(1, [0])
            logits(0, 0)
            variance(2)
            make_k(1, [1])
            with dve.Fori(0, BATCH - 2) as b:
                step(b, True, True)
            step(BATCH - 2, True, False)
            step(BATCH - 1, False, False)

        @block.scalar
        def _(act):
            def left_row(b, r, turns):
                base = work_base(b) + TURN_AT[r]
                if r == 2 and not (isinstance(b, int) and b == 0):
                    act.wait_ge(s_stored, 16 * (2 * b - 1))
                for g in range(TURNS[r])[turns]:
                    w = (min(4 * g + 4, r) - 4 * g) * P
                    at = LEFT_AT[r % LEFTS] + g * CHUNK
                    k = TURN_AT[r] + g
                    act.wait_ge(s_filled, base + g + 1)
                    nc.scalar.activation(left[:, at:at + w], bank(k)[:, 0:w], ACT.Identity,
                                         accum_out=deg_part[:, 6 * r + 2 + g:6 * r + 3 + g]).then_inc(s_drained, 1)

            def scale_row(b, r):
                if r == 0:
                    act.wait_ge(s_norm, 2 * b + 1)
                act.wait_ge(s_deg, TILES * b + r + 1)
                if r >= 2:
                    act.wait_ge(s_mm0, TILES * b + r - 1)
                nc.scalar.activation(scaled[r % 2][:, :], x_norm[:, r * CH:(r + 1) * CH], ACT.Relu,
                                     scale=deg_inv[:, r:r + 1]).then_inc(s_scaled, 1)

            def row_begin(b, r):
                if r < TILES:
                    left_row(b, r, FIRST)
                if r >= 2:
                    scale_row(b, r - 2)

            def row_end(b, r):
                if r < TILES:
                    left_row(b, r, REST)

            def agg_out(b):
                act.wait_ge(s_mm0, TILES * (b + 1))
                nc.scalar.activation(left[:, AGG_T:AGG_T + ROW], acc0[:, :], ACT.Copy).then_inc(s_agg, 1)

            def to_nodes(dest, n_static, m):
                d = dest[:, m * HALF:(m + 1) * HALF].rearrange("p (h k c) -> p k h c", h=2, c=CH)
                s = bank(n_static).rearrange("p (k h c) -> p k h c", k=4, c=CH)
                return d, s

            def agg_back(b):
                for m in range(2):
                    act.wait_ge(s_filled, work_base(b) + W_AGG + m + 1)
                    d, s = to_nodes(x_norm, W_AGG + m, m)
                    nc.scalar.activation(d, s, ACT.Copy).then_inc(s_drained, 1)

            def square(n):
                act.wait_ge(s_cent, n + 1)
                nc.scalar.activation(left[:, AGG_T:AGG_T + ROW], x_norm[:, :], ACT.Square).then_inc(s_sq, 1)

            def activ_t(b):
                for m in range(2):
                    act.wait_ge(s_filled, work_base(b) + W_XN + m + 1)
                    nc.scalar.activation(left[:, ACTIV_T + m * HALF:ACTIV_T + (m + 1) * HALF], bank(W_XN + m),
                                         ACT.Relu).then_inc(s_drained, 1)

            def hidden_t_out(b):
                for m in range(2):
                    act.wait_ge(s_filled, work_base(b) + W_HID + m + 1)
                    nc.scalar.activation(left[:, LEAKY_T + m * HALF:LEAKY_T + (m + 1) * HALF], bank(W_HID + m),
                                         ACT.Copy).then_inc(s_drained, 1)

            def src_out(b):
                if not (isinstance(b, int) and b == 0):
                    act.wait_ge(s_t, TILES * b)
                row = src_row[:, :].rearrange("p (q two n) -> p two q n", two=2, n=P)
                for k in range(4):
                    act.wait_ge(s_filled, work_base(b) + W_SRC + k + 1)
                    nc.scalar.activation(row[:, k // 2, 4 * (k % 2):4 * (k % 2) + 4, :],
                                         bank(W_SRC + k).rearrange("p (q n) -> p q n", n=P), ACT.Copy,
                                         scale=0.25).then_inc(s_drained, 1)

            def dst_out(b):
                if not (isinstance(b, int) and b == 0):
                    act.wait_ge(s_p, CHUNKS * TILES * b)
                for m in range(2):
                    act.wait_ge(s_filled, work_base(b) + W_DST + m + 1)
                    nc.scalar.activation(dst[:, m * 8:(m + 1) * 8], bank(W_DST + m)[:, 0:8], ACT.Copy,
                                         scale=0.2).then_inc(s_drained, 1)

            def exponentials(b, j, chunks):
                act.wait_ge(s_t, TILES * b + j + 1)
                for q in chunks:
                    if j > 0 or q >= 2:
                        act.wait_ge(s_p, CHUNKS * (TILES * b + j) + q - 1)
                    nc.scalar.activation(exps[:, (q % 2) * CHUNK:(q % 2 + 1) * CHUNK],
                                         adjt[j % ADJT_SLOTS][:, q * CHUNK:(q + 1) * CHUNK], ACT.Exp,
                                         bias=low[:, j:j + 1], scale=-1.0).then_inc(s_e, 1)

            def weigh(b, j):
                if j == 0:
                    act.wait_ge(s_drained, work_base(b) + W_NAT + 2)
                act.wait_ge(s_z, TILES * b + j + 1)
                if j >= 2:
                    act.wait_ge(s_mm1, TILES * b + j - 1)
                nc.scalar.activation(weighed[j % 2][:, :], hidden[:, j * CH:(j + 1) * CH], ACT.Copy,
                                     scale=total[:, j:j + 1]).then_inc(s_hz, 1)

            def acc1_out(b):
                act.wait_ge(s_acc1, b + 1)
                nc.scalar.activation(left[:, LEAKY_T:LEAKY_T + ROW], acc1[:, :], ACT.Copy).then_inc(s_hpt, 1)

            def hidden_out(b):
                for m in range(2):
                    act.wait_ge(s_filled, work_base(b) + W_NAT + m + 1)
                    nc.scalar.activation(hidden[:, m * HALF:(m + 1) * HALF], bank(W_NAT + m),
                                         ACT.Copy).then_inc(s_drained, 1)

            def relu_out(base, k):
                for m in range(2):
                    act.wait_ge(s_filled, base + k + m + 1)
                    d, s = to_nodes(left[:, AGG_T:AGG_T + ROW], k + m, m)
                    nc.scalar.activation(d, s, ACT.Relu).then_inc(s_drained, 1)

            def step(b, l0, more):
                for j in range(1, TILES):
                    rows = ROWS_AT.get(j, []) if l0 else []
                    if l0 and j == J_AGG:
                        agg_out(b + 1)
                    if l0 and j == J_CENTER:
                        square(2 * (b + 1) + 1)
                    if l0 and j == J_TURN:
                        activ_t(b + 1)
                    if j >= 2:
                        weigh(b, j - 2)
                    if rows:
                        row_begin(b + 1, rows[0])
                    exponentials(b, j - 1, (2, 3))
                    if rows:
                        row_end(b + 1, rows[0])
                    for r in rows[1:]:
                        row_begin(b + 1, r)
                    exponentials(b, j, (0, 1))
                    for r in rows[1:]:
                        row_end(b + 1, r)
                    if l0 and j == J_TURN:
                        hidden_t_out(b + 1)
                    if l0 and j == J_AGG:
                        agg_back(b + 1)
                weigh(b, TILES - 2)
                exponentials(b, TILES - 1, (2, 3))
                if l0:
                    src_out(b + 1)
                weigh(b, TILES - 1)
                if l0:
                    dst_out(b + 1)
                if more:
                    square(2 * (b + 2))
                if l0:
                    exponentials(b + 1, 0, (0, 1))
                    act.wait_ge(s_lsm, b + 1)
                    hidden_out(b + 1)
                if more:
                    act.wait_ge(s_var, 2 * (b + 2) + 1)
                acc1_out(b)
                relu_out(work_base(b + 1), W_OUT if l0 else 0)

            k = 0
            for r in range(TILES):
                for c in range(r, TILES, 4):
                    w = (min(c + 4, TILES) - c) * P
                    act.wait_ge(s_filled, k + 1)
                    at = GATE_AT[r] + (c - r) * P
                    nc.scalar.activation(gate[:, at:at + w], bank(k)[:, 0:w], ACT.Sigmoid).then_inc(s_drained, 1)
                    k += 1
            square(0)
            for r in range(1, TILES + 2):
                row_begin(0, r)
                row_end(0, r)
            agg_out(0)
            agg_back(0)
            square(1)
            activ_t(0)
            hidden_t_out(0)
            src_out(0)
            dst_out(0)
            square(2)
            exponentials(0, 0, (0, 1))
            hidden_out(0)
            with act.Fori(0, BATCH - 2) as b:
                step(b, True, True)
            step(BATCH - 2, True, False)
            step(BATCH - 1, False, False)

        @block.tensor
        def _(pe):
            def free_bank(n):
                pe.wait_ge(s_drained, n - 1)

            def turn_row(b, r, turns):
                pe.wait_ge(s_k, len(UNITS) * b + UNITS_OF[r - 1][-1] + 1)
                for g in range(TURNS[r])[turns]:
                    k = TURN_AT[r] + g
                    free_bank(work_base(b) + k)
                    for c in range(4 * g, min(4 * g + 4, r)):
                        at = K_AT[c] + (r - c) * P
                        t = pe.transpose(bank(k)[:, (c % 4) * P:(c % 4 + 1) * P], k_rows[:, at:at + P], ident)
                    t.then_inc(s_filled, 1)

            def multiply_row(b, r, chunks):
                pe.wait_ge(s_scaled, TILES * b + r + 1)
                if r == 0 and not (isinstance(b, int) and b == 0):
                    pe.wait_ge(s_agg, b)
                for q in chunks:
                    lo, hi = q * CHUNK, (q + 1) * CHUNK
                    mid = min(max(r * P, lo), hi)
                    acc = chunk_of(acc0, q)
                    lw = scaled[r % 2][:, :]
                    parts = []
                    if lo < mid:
                        at = LEFT_AT[r % LEFTS]
                        parts.append((lo, mid, left[:, at + lo:at + mid]))
                    if mid < hi:
                        at = K_AT[r] - r * P
                        parts.append((mid, hi, k_rows[:, at + mid:at + hi]))
                    for n, (a, z, rhs) in enumerate(parts):
                        m = pe.matmul(acc[:, a - lo:z - lo], lw, rhs, start=(r == 0),
                                      stop=(r == TILES - 1 and n == len(parts) - 1))
                if CHUNKS - 1 in chunks:
                    m.then_inc(s_mm0, 1)

            def row(b, r, between=None):
                if r < TILES:
                    turn_row(b, r, FIRST)
                if between is not None:
                    between()
                elif r >= 2:
                    multiply_row(b, r - 2, (0, 1))
                if r < TILES and TURNS[r] > 2:
                    turn_row(b, r, REST)
                if r >= 2:
                    multiply_row(b, r - 2, range(CHUNKS) if between is not None else (2, 3))

            def turn_back(base, k0, region):
                for m in range(2):
                    free_bank(base + k0 + m)
                    for k in range(4):
                        at = region + (4 * m + k) * P
                        t = pe.transpose(bank(k0 + m)[:, k * P:(k + 1) * P], left[:, at:at + P], ident)
                    t.then_inc(s_filled, 1)

            def turn_norm(b):
                pe.wait_ge(s_norm, 2 * b + 2)
                for m in range(2):
                    free_bank(work_base(b) + W_XN + m)
                    for k in range(4):
                        q = 4 * m + k
                        t = pe.transpose(bank(W_XN + m)[:, k * P:(k + 1) * P], x_norm[:, q * P:(q + 1) * P], ident)
                    t.then_inc(s_filled, 1)

            def hidden_t(b):
                pe.wait_ge(s_drained, work_base(b) + W_XN + 2)
                for m in range(2):
                    free_bank(work_base(b) + W_HID + m)
                    pe.matmul(bank(W_HID + m), w_pair, left[:, ACTIV_T + m * HALF:ACTIV_T + (m + 1) * HALF],
                              start=True, stop=True).then_inc(s_filled, 1)

            def src_and_dst(b):
                pe.wait_ge(s_leaky, b + 1)
                for k in range(4):
                    free_bank(work_base(b) + W_SRC + k)
                    at = LEAKY_T + (k % 2) * HALF
                    pe.matmul(bank(W_SRC + k), cst[:, C_SRC + (k // 2) * P:C_SRC + (k // 2 + 1) * P],
                              left[:, at:at + HALF], start=True, stop=True).then_inc(s_filled, 1)
                for m in range(2):
                    free_bank(work_base(b) + W_DST + m)
                    for k in range(4):
                        at = LEAKY_T + (4 * m + k) * P
                        t = pe.matmul(bank(W_DST + m)[:, 2 * k:2 * k + 2], left[:, at:at + P],
                                      cst[:, C_DST:C_DST + 2], start=True, stop=True)
                    t.then_inc(s_filled, 1)

            def hidden_nodes(b):
                for m in range(2):
                    free_bank(work_base(b) + W_NAT + m)
                    for k in range(4):
                        at = ACTIV_T + (4 * m + k) * P
                        t = pe.matmul(bank(W_NAT + m)[:, k * P:(k + 1) * P], left[:, at:at + P], w_pair,
                                      start=True, stop=True)
                    t.then_inc(s_filled, 1)

            def gather_row(b, j):
                pe.wait_ge(s_hz, TILES * b + j + 1)
                for q in range(CHUNKS):
                    m = pe.matmul(chunk_of(acc1, q), weighed[j % 2][:, :],
                                  adjt[j % ADJT_SLOTS][:, q * CHUNK:(q + 1) * CHUNK], start=(j == 0), stop=False)
                m.then_inc(s_mm1, 1)

            def gather_lone(b):
                pe.wait_ge(s_lsm, b + 1)
                for q in range(CHUNKS):
                    m = pe.matmul(chunk_of(acc1, q), lone_sum[:, :], uniform[:, 0:1].to_broadcast([P, CHUNK]),
                                  start=False, stop=True)
                m.then_inc(s_acc1, 1)

            def step(b, l0, more):
                for j in range(1, TILES):
                    rows = ROWS_AT.get(j, []) if l0 else []
                    if l0 and j == J_TURN:
                        turn_norm(b + 1)
                    gather = (lambda: gather_row(b, j - 2)) if j >= 2 else None
                    if rows:
                        row(b + 1, rows[0], gather)
                    elif gather is not None:
                        gather()
                    for r in rows[1:]:
                        row(b + 1, r)
                    if l0 and j == J_AGG:
                        pe.wait_ge(s_agg, b + 2)
                        turn_back(work_base(b + 1), W_AGG, AGG_T)
                    if l0 and j == J_TURN:
                        hidden_t(b + 1)
                    if l0 and j == TILES - 1:
                        src_and_dst(b + 1)
                gather_row(b, TILES - 2)
                gather_row(b, TILES - 1)
                if l0:
                    hidden_nodes(b + 1)
                gather_lone(b)
                pe.wait_ge(s_hpt, b + 1)
                turn_back(work_base(b + 1), W_OUT if l0 else 0, LEAKY_T)

            pe.wait_ge(s_u, 16)
            k = 0
            for r in range(TILES):
                for c in range(r, TILES, 4):
                    w = (min(c + 4, TILES) - c) * P
                    if k >= 2:
                        free_bank(k)
                    pe.matmul(bank(k)[:, 0:w], u_sb[:, r * P:(r + 1) * P], u_sb[:, c * P:c * P + w],
                              start=True, stop=True).then_inc(s_filled, 1)
                    k += 1
            pe.wait_ge(s_cst, 16)
            pe.wait_ge(s_const, 2)
            for r in range(1, TILES + 2):
                row(0, r)
            pe.wait_ge(s_agg, 1)
            turn_back(work_base(0), W_AGG, AGG_T)
            turn_norm(0)
            hidden_t(0)
            src_and_dst(0)
            hidden_nodes(0)
            with pe.Fori(0, BATCH - 2) as b:
                step(b, True, True)
            step(BATCH - 2, True, False)
            step(BATCH - 1, False, False)


def kernel(x, adj, L0_gnn_U, L0_gnn_w_scale, L1_gnn_W, L1_gnn_a):
    import concourse.bacc as bacc
    from concourse.bass_utils import run_bass_kernel_spmd

    x, adj, u, w_scale, w, a = (np.asarray(v) for v in (x, adj, L0_gnn_U, L0_gnn_w_scale, L1_gnn_W, L1_gnn_a))
    rows = np.ascontiguousarray(x.reshape(BATCH, TILES, P, CH).transpose(0, 2, 1, 3).reshape(BATCH, P, ROW))
    adj_t = np.ascontiguousarray(adj.transpose(0, 2, 1)).reshape(BATCH, TILES, P, NODES)
    tiled = adj.reshape(BATCH, TILES, P, NODES)
    pairs = np.empty((BATCH, P, PAIR_ROW), np.float32)
    for n, (r, c0, c1) in enumerate(UNITS):
        mid = (PAIR_AT[n] + PAIR_AT[n + 1]) // 2
        pairs[:, :, PAIR_AT[n]:mid] = tiled[:, r, :, c0 * P:c1 * P]
        pairs[:, :, mid:PAIR_AT[n + 1]] = adj_t[:, r, :, c0 * P:c1 * P]
    consts = np.zeros((P, C_COLS), np.float32)
    consts[:, C_ID:C_ID + P] = np.eye(P, dtype=np.float32)
    for half in range(2):
        at = slice(half * CH, (half + 1) * CH)
        consts[at, C_W + half * CH:C_W + (half + 1) * CH] = w
        consts[at, C_SRC + half * P:C_SRC + (half + 1) * P] = a[:CH]
        consts[at, C_DST + half] = a[CH:, 0]
    consts[:, C_SCALE] = w_scale
    arrays = {"x_rows": rows, "adj_pairs": pairs, "adj_t": adj_t, "u_t": np.ascontiguousarray(u.T), "consts": consts}
    nc = bacc.Bacc("TRN2", target_bir_lowering=False, num_devices=1, dynamic_dma_scratch_size=1024)
    aps = [nc.dram_tensor(name, v.shape, F32, kind="ExternalInput").ap() for name, v in arrays.items()]
    out = nc.dram_tensor("out_rows", (BATCH, P, ROW), F32, kind="ExternalOutput").ap()
    x1_store = nc.dram_tensor("x1_store", (BATCH, P, ROW), F32, kind="Internal").ap()
    gnn_program(nc, *aps, x1_store, out)
    got = run_bass_kernel_spmd(nc, [arrays], core_ids=[0]).results[0]["out_rows"]
    return np.ascontiguousarray(got.reshape(BATCH, P, TILES, CH).transpose(0, 2, 1, 3).reshape(BATCH, NODES, CH))
```

```python
from contextlib import ExitStack

import numpy as np
import concourse.bass as bass
from concourse import mybir

F32 = mybir.dt.float32
ALU = mybir.AluOpType
ACT = mybir.ActivationFunctionType
AX_X = mybir.AxisListType.X

P = 128
BATCH, NODES, CH, RANK = 8, 2048, 64, 16
TILES = NODES // P
ROW = TILES * CH
CHUNK = 512
CHUNKS = NODES // CHUNK
HALF = ROW // 2
TINY = 1e-12
LONE_STEPS = TILES.bit_length() - 1

UNIT = 8
UNITS = [(r, c, min(c + UNIT, TILES)) for r in range(TILES) for c in range(r, TILES, UNIT)]
UNITS_OF = [[n for n, (row, _, _) in enumerate(UNITS) if row == r] for r in range(TILES)]
PAIR_SLOTS = 3
ADJT_SLOTS = 4
assert len(UNITS) % PAIR_SLOTS == 0 and TILES % ADJT_SLOTS == 0
PAIR_AT = np.cumsum([0] + [2 * (c1 - c0) * P for _, c0, c1 in UNITS]).tolist()
PAIR_ROW = PAIR_AT[-1]

GATE_AT = np.cumsum([0] + [(TILES - r) * P for r in range(TILES)]).tolist()
K_AT = GATE_AT[:8] * 2
K_ROW = GATE_AT[8]
LEFTS = 3
LEFT_MAX = [max(r for r in range(TILES) if r % LEFTS == n) for n in range(LEFTS)]
LEFT_AT = np.cumsum([0] + [blocks * P for blocks in LEFT_MAX]).tolist()
LEFT_ROW = LEFT_AT[-1]
AGG_T, ACTIV_T, LEAKY_T, X1_NEW = 0, ROW, 3 * ROW, 4 * ROW
assert X1_NEW + ROW <= LEFT_ROW

TURNS = [-(-r // 4) for r in range(TILES)]
FIRST, REST = slice(0, 2), slice(2, None)
TURN_AT = np.cumsum([0] + TURNS).tolist()
W_AGG = TURN_AT[-1]
W_XN = W_AGG + 2
W_HID = W_XN + 2
W_SRC = W_HID + 2
W_DST = W_SRC + 4
W_NAT = W_DST + 2
W_OUT = W_NAT + 2
W_STEP = W_OUT + 2
GATE_TURNS_BY = np.cumsum([-(-(TILES - r) // 4) for r in range(TILES)]).tolist()
W_GATES = sum(-(-(TILES - r) // 4) for r in range(TILES))
assert W_GATES % 2 == 0 and W_STEP % 2 == 0

ROWS_AT = {1: [1, 2], 2: [3, 4], 3: [5, 6], 4: [7, 8], 5: [9, 10], 6: [11, 12], 7: [13, 14],
           8: [15, 16], 9: [17]}
K_IN = {r: [r] if r >= UNIT else [r + 1] if r + 1 < UNIT else [] for r in range(TILES)}
SUM_IN = {r: UNITS_OF[r + 1] for r in range(UNIT - 1, TILES - 1)} | {2: [11, 12], 3: [13, 14], 4: [15]}
SUMS_AHEAD_AT = {8: [0], 9: [1], 10: [2], 11: [3], 12: [4], 13: [5, 6], 14: [7], 15: [8]}
SUMS_AHEAD_END = [9, 10]
AHEAD = min(min(units) for units in SUM_IN.values())
J_AGG, J_X1, J_CENTER, J_NORM, J_TURN, J_NEXT = 10, 11, 12, 13, 14, 14

C_ID, C_W, C_SRC, C_DST, C_SCALE = 0, P, 2 * P, 2 * P + 2, 2 * P + 4
C_COLS = C_SCALE + 1


def work_base(b):
    return W_GATES if isinstance(b, int) and b == 0 else W_GATES + W_OUT + W_STEP * (b - 1)


def gnn_program(nc, x, pairs, adj_t, u_t, consts, out):
    with ExitStack() as ctx:
        def sb(name, cols, parts=P):
            return ctx.enter_context(nc.sbuf_tensor(name, [parts, cols], F32))

        def sem(name):
            return ctx.enter_context(nc.semaphore(name))

        gate = sb("gate", GATE_AT[-1])
        k_rows = sb("k_rows", K_ROW)
        left = sb("left", LEFT_ROW)
        pair = [sb(f"pair{i}", 2 * UNIT * P) for i in range(PAIR_SLOTS)]
        adjt = [sb(f"adjt{i}", NODES) for i in range(ADJT_SLOTS)]
        src_row = sb("src_row", NODES)
        x_in = sb("x_in", ROW)
        x_norm = sb("x_norm", ROW)
        x1 = sb("x1", ROW)
        hidden = sb("hidden", ROW)
        cst = sb("cst", C_COLS)
        scaled = [sb(f"scaled{i}", CH) for i in range(2)]
        weighed = [sb(f"weighed{i}", CH) for i in range(2)]
        deg_part = sb("deg_part", TILES * 6)
        deg = sb("deg", TILES)
        deg_inv = sb("deg_inv", TILES)
        deg_out = sb("deg_out", TILES)
        minus_half = sb("minus_half", TILES)
        ln_mean = sb("ln_mean", TILES)
        ln_var = sb("ln_var", TILES)
        low = sb("low", TILES)
        dst = sb("dst", TILES)
        flag = sb("flag", TILES)
        part_sum = sb("part_sum", TILES * 4)
        total_sum = sb("total_sum", TILES)
        total_inv = sb("total_inv", TILES)
        summed = sb("summed", CHUNKS)
        lone_sum = sb("lone_sum", CH)
        uniform = sb("uniform", 1)
        one = sb("one", 1)
        u_sb = src_row[0:RANK, :]

        acc0 = ctx.enter_context(nc.psum_tensor("acc0", [P, 2 * CHUNK], F32))
        acc1 = ctx.enter_context(nc.psum_tensor("acc1", [P, 2 * CHUNK], F32))
        exps = ctx.enter_context(nc.psum_tensor("exps", [P, 2 * CHUNK], F32))
        work = ctx.enter_context(nc.psum_tensor("work", [P, 2 * CHUNK], F32))

        s_cst = sem("consts_loaded")
        s_u = sem("u_loaded")
        s_zero = sem("u_padded")
        s_pair = [sem(f"pair_loaded{i}") for i in range(PAIR_SLOTS)]
        s_adjt = [sem(f"adjt_loaded{i}") for i in range(ADJT_SLOTS)]
        s_x = sem("x_loaded")
        s_stored = sem("out_stored")
        s_const = sem("small_consts_set")
        s_filled = sem("work_filled")
        s_drained = sem("work_drained")
        s_sum = sem("pairs_summed")
        s_k = sem("k_units_made")
        s_degp = sem("degrees_summed")
        s_degc = sem("degrees_clamped")
        s_deg = sem("degrees_inverted")
        s_scaled = sem("scaled_rows_made")
        s_mm0 = sem("layer0_rows_multiplied")
        s_agg = sem("agg_copied")
        s_dw = sem("deg_out_made")
        s_aggs = sem("agg_scaled")
        s_x1 = sem("x1_made")
        s_x1m = sem("x1_moved")
        s_lsum = sem("ln_summed")
        s_mean = sem("ln_mean_made")
        s_cent = sem("ln_centered")
        s_sq = sem("ln_squared")
        s_vsum = sem("ln_squares_summed")
        s_var = sem("ln_var_made")
        s_rstd = sem("ln_rstd_made")
        s_norm = sem("ln_normed")
        s_leaky = sem("leaky_made")
        s_begun = sem("logits_begun")
        s_t = sem("logits_made")
        s_e = sem("exp_chunks_made")
        s_p = sem("masked_chunks_made")
        s_z1 = sem("totals_summed")
        s_z = sem("totals_inverted")
        s_hz = sem("weighed_rows_made")
        s_mm1 = sem("layer1_rows_multiplied")
        s_flag = sem("lone_flags_made")
        s_lone = sem("lone_hidden_made")
        s_lsm = sem("lone_sum_made")
        s_acc1 = sem("acc1_complete")
        s_hpt = sem("acc1_copied")
        s_out = sem("out_made")

        ident = cst[:, C_ID:C_ID + P]
        w_pair = cst[:, C_W:C_W + P]

        def bank(n):
            return work[:, (n % 2) * CHUNK:(n % 2 + 1) * CHUNK]

        def gate_bank(k):
            two = work if k % 4 < 2 else exps
            return two[:, (k % 2) * CHUNK:(k % 2 + 1) * CHUNK]

        def tch(ap):
            return ap.rearrange("p (t c) -> p t c", c=CH)

        def per_tile(col):
            return col[:, :].unsqueeze(2).to_broadcast([P, TILES, CH])

        def chunk_of(acc, q):
            return acc[CH * (q % 2):CH * (q % 2) + CH, (q // 2) * CHUNK:(q // 2 + 1) * CHUNK]

        x1_next = left[:, X1_NEW:X1_NEW + ROW]

        block = ctx.enter_context(nc.Block())

        @block.sync
        def _(sp):
            def load_pair(b, n):
                sp.dma_start(pair[n % PAIR_SLOTS][:, 0:PAIR_AT[n + 1] - PAIR_AT[n]],
                             pairs[b, :, PAIR_AT[n]:PAIR_AT[n + 1]]).then_inc(s_pair[n % PAIR_SLOTS], 16)

            def load_pairs_behind(b, units, last):
                for n in units:
                    if n + PAIR_SLOTS < len(UNITS):
                        sp.wait_ge(s_sum, len(UNITS) * b + n + 1)
                        load_pair(b, n + PAIR_SLOTS)
                    elif not last:
                        sp.wait_ge(s_sum, len(UNITS) * b + n + 1)
                        load_pair(b + 1, n + PAIR_SLOTS - len(UNITS))

            def load_adjt(b, j):
                sp.dma_start(adjt[j % ADJT_SLOTS][:, :], adj_t[b, j, :, :]).then_inc(s_adjt[j % ADJT_SLOTS], 16)

            def load_adjt_behind(b, j, last):
                nxt = j + ADJT_SLOTS
                if nxt < TILES:
                    sp.wait_ge(s_mm1, TILES * b + j + 1)
                    load_adjt(b, nxt)
                elif not last:
                    sp.wait_ge(s_mm1, TILES * b + j + 1)
                    load_adjt(b + 1, nxt - TILES)

            def load_x(b):
                sp.dma_start(x_in[:, :], x[b, :, :]).then_inc(s_x, 16)

            def step(b, l0, more):
                for j in range(1, TILES):
                    if l0:
                        load_pairs_behind(b + 1, [n for r in ROWS_AT.get(j, []) for n in SUM_IN.get(r, [])], not more)
                    if j >= 2:
                        load_adjt_behind(b, j - 2, not l0)
                    if more:
                        load_pairs_behind(b + 2, SUMS_AHEAD_AT.get(j, []), False)
                    if j == J_CENTER and more:
                        sp.wait_ge(s_x1, b + 2)
                        load_x(b + 2)
                load_adjt_behind(b, TILES - 2, not l0)
                if more:
                    load_pairs_behind(b + 2, SUMS_AHEAD_END[:1], False)
                if l0:
                    load_adjt_behind(b, TILES - 1, False)
                if more:
                    load_pairs_behind(b + 2, SUMS_AHEAD_END[1:], False)
                sp.wait_ge(s_out, b + 1)
                sp.dma_start(out[b, :, :], left[:, AGG_T:AGG_T + ROW]).then_inc(s_stored, 16)

            load_pair(0, 0)
            sp.wait_ge(s_zero, 1)
            sp.dma_start(u_sb, u_t[:, :]).then_inc(s_u, 16)
            load_x(0)
            for n in range(1, PAIR_SLOTS):
                load_pair(0, n)
            sp.dma_start(cst[:, :], consts[:, :]).then_inc(s_cst, 16)
            load_pairs_behind(0, range(len(UNITS)), False)
            load_pairs_behind(1, UNITS_OF[0], False)
            for j in range(ADJT_SLOTS):
                load_adjt(0, j)
            sp.wait_ge(s_x1, 1)
            load_x(1)
            load_pairs_behind(1, range(len(UNITS_OF[0]), AHEAD), False)
            with sp.Fori(0, BATCH - 2) as b:
                step(b, True, True)
            step(BATCH - 2, True, False)
            step(BATCH - 1, False, False)
            sp.wait_ge(s_stored, 16 * (BATCH + 1))

        @block.gpsimd
        def _(pool):
            def sum_unit(b, n):
                r, c0, c1 = UNITS[n]
                first = n == UNITS_OF[r][0]
                again = not (isinstance(b, int) and b == 0)
                if r >= UNIT:
                    if r == UNIT:
                        pool.wait_ge(s_filled, work_base(b) + TURN_AT[UNIT])
                    pool.wait_ge(s_mm0, TILES * b + r - UNIT + 1)
                elif r == 0 and first and again:
                    pool.wait_ge(s_filled, work_base(b - 1) + TURN_AT[TILES])
                    pool.wait_ge(s_mm0, TILES * b - 3)
                elif r == 5 and first and again:
                    pool.wait_ge(s_mm0, TILES * b)
                pool.wait_ge(s_pair[n % PAIR_SLOTS], 16 * (len(UNITS) // PAIR_SLOTS * b + n // PAIR_SLOTS + 1))
                at, w = K_AT[r] + (c0 - r) * P, (c1 - c0) * P
                p = pair[n % PAIR_SLOTS]
                nc.gpsimd.tensor_tensor(k_rows[:, at:at + w], p[:, 0:w], p[:, w:2 * w], ALU.add).then_inc(s_sum, 1)

            def sum_row(b, r):
                for n in UNITS_OF[r]:
                    sum_unit(b, n)

            def invert_degree(b, r):
                pool.wait_ge(s_degc, TILES * b + r + 1)
                nc.gpsimd.tensor_tensor(deg_inv[:, r:r + 1], deg[:, r:r + 1], minus_half[:, r:r + 1],
                                        ALU.pow).then_inc(s_deg, 1)

            def row(b, r, units):
                if r >= 2:
                    invert_degree(b, r - 2)
                for n in units:
                    sum_unit(b, n)

            def add_layer0(b):
                pool.wait_ge(s_deg, TILES * (b + 1))
                nc.gpsimd.tensor_tensor(deg_out[:, :], deg_inv[:, :],
                                        cst[:, C_SCALE:C_SCALE + 1].to_broadcast([P, TILES]), ALU.mult).then_inc(s_dw, 1)
                pool.wait_ge(s_dw, b + 1)
                pool.wait_ge(s_drained, work_base(b) + W_AGG + 2)
                nc.gpsimd.tensor_tensor(tch(x_norm[:, :]), tch(x_norm[:, :]), per_tile(deg_out),
                                        ALU.mult).then_inc(s_aggs, 1)
                pool.wait_ge(s_aggs, b + 1)
                nc.gpsimd.tensor_tensor(x1_next, x_norm[:, :], x_in[:, :], ALU.add).then_inc(s_x1, 1)

            def center(n, source):
                pool.wait_ge(s_mean, n + 1)
                nc.gpsimd.tensor_tensor(tch(x_norm[:, :]), tch(source), per_tile(ln_mean),
                                        ALU.subtract).then_inc(s_cent, 1)

            def normalize(n):
                pool.wait_ge(s_var, n + 1)
                nc.gpsimd.tensor_tensor(ln_var[:, :], ln_var[:, :], minus_half[:, :], ALU.pow).then_inc(s_rstd, 1)
                pool.wait_ge(s_rstd, n + 1)
                nc.gpsimd.tensor_tensor(tch(x_norm[:, :]), tch(x_norm[:, :]), per_tile(ln_var),
                                        ALU.mult).then_inc(s_norm, 1)

            def lone(b):
                pool.wait_ge(s_flag, b + 1)
                pool.wait_ge(s_hz, TILES * (b + 1))
                nc.gpsimd.tensor_tensor(tch(hidden[:, :]), tch(hidden[:, :]), per_tile(flag),
                                        ALU.mult).then_inc(s_lone, 1)
                n, w = 0, HALF
                while w >= CH:
                    pool.wait_ge(s_lone, LONE_STEPS * b + n + 1)
                    d = lone_sum[:, :] if w == CH else hidden[:, 0:w]
                    nc.gpsimd.tensor_tensor(d, hidden[:, 0:w], hidden[:, w:2 * w],
                                            ALU.add).then_inc(s_lsm if w == CH else s_lone, 1)
                    n, w = n + 1, w // 2

            def add_layer1(b, relu_at):
                pool.wait_ge(s_drained, relu_at)
                res = left[:, AGG_T:AGG_T + ROW]
                nc.gpsimd.tensor_tensor(res, res, x1[:, :], ALU.add).then_inc(s_out, 1)

            def move_x1(b):
                if isinstance(b, int):
                    pool.wait_ge(s_out, b)
                else:
                    pool.wait_ge(s_sum, len(UNITS) * (b + 1) + SUM_IN[4][-1] + 1)
                nc.gpsimd.tensor_tensor(x1[:, :], x1_next, one[:, 0:1].to_broadcast([P, ROW]),
                                        ALU.mult).then_inc(s_x1m, 1)

            def step(b, l0, more):
                for j in range(1, TILES):
                    if l0:
                        for r in ROWS_AT.get(j, []):
                            row(b + 1, r, SUM_IN.get(r, []))
                    if j == 2:
                        move_x1(b)
                    if l0:
                        if j == J_X1:
                            add_layer0(b + 1)
                        if j == J_CENTER:
                            center(2 * (b + 1) + 1, x1_next)
                        if j == J_NORM:
                            normalize(2 * (b + 1) + 1)
                    if more:
                        for n in SUMS_AHEAD_AT.get(j, []):
                            sum_unit(b + 2, n)
                if more:
                    pool.wait_ge(s_filled, work_base(b + 1) + W_XN + 2)
                    center(2 * (b + 2), x_in[:, :])
                if more:
                    sum_unit(b + 2, SUMS_AHEAD_END[0])
                lone(b)
                if more:
                    sum_unit(b + 2, SUMS_AHEAD_END[1])
                    normalize(2 * (b + 2))
                add_layer1(b, work_base(b + 1) + (W_STEP if l0 else 2))

            nc.gpsimd.memset(minus_half[:, :], -0.5).then_inc(s_const, 1)
            nc.gpsimd.memset(one[:, :], 1.0).then_inc(s_const, 1)
            pool.wait_ge(s_const, 3)
            center(0, x_in[:, :])
            sum_row(0, 0)
            normalize(0)
            sum_row(0, 1)
            sum_row(0, 2)
            for r in range(2, TILES + 2):
                if r + 1 < UNIT:
                    sum_row(0, r + 1)
                row(0, r, UNITS_OF[r + 1] if r + 1 in range(UNIT, TILES) else [])
            pool.wait_ge(s_cst, 16)
            sum_row(1, 0)
            add_layer0(0)
            center(1, x1_next)
            sum_row(1, 1)
            normalize(1)
            sum_row(1, 2)
            sum_row(1, 3)
            pool.wait_ge(s_filled, work_base(0) + W_XN + 2)
            center(2, x_in[:, :])
            sum_row(1, 4)
            normalize(2)
            sum_unit(1, AHEAD - 1)
            with pool.Fori(0, BATCH - 2) as b:
                step(b, True, True)
            step(BATCH - 2, True, False)
            step(BATCH - 1, False, False)

        @block.vector
        def _(dve):
            def k_unit(b, n):
                r, c0, c1 = UNITS[n]
                dve.wait_ge(s_sum, len(UNITS) * b + n + 1)
                if isinstance(b, int) and b == 0:
                    dve.wait_ge(s_drained, GATE_TURNS_BY[r])
                at, w = (c0 - r) * P, (c1 - c0) * P
                col = 6 * r + (1 if r >= UNIT or c0 > r else 0)
                k = k_rows[:, K_AT[r] + at:K_AT[r] + at + w]
                nc.vector.tensor_tensor_reduce(k, k,
                                               gate[:, GATE_AT[r] + at:GATE_AT[r] + at + w],
                                               0.5, 0.0, ALU.mult, ALU.add,
                                               deg_part[:, col:col + 1]).then_inc(s_k, 1)

            def degree(b, r):
                if r >= 1:
                    dve.wait_ge(s_drained, work_base(b) + TURN_AT[r] + TURNS[r])
                dve.wait_ge(s_k, len(UNITS) * b + UNITS_OF[r][-1] + 1)
                first = 6 * r + (1 if r >= UNIT else 0)
                nc.vector.tensor_reduce(deg[:, r:r + 1], deg_part[:, first:6 * r + 2 + TURNS[r]], AX_X,
                                        ALU.add).then_inc(s_degp, 1)
                dve.wait_ge(s_degp, TILES * b + r + 1)
                nc.vector.tensor_scalar(deg[:, r:r + 1], deg[:, r:r + 1], 1e-12, None, ALU.max).then_inc(s_degc, 1)

            def make_k(b, rows):
                for r in rows:
                    for n in UNITS_OF[r]:
                        k_unit(b, n)

            def mean(n, source):
                nc.vector.tensor_reduce(ln_mean[:, :], tch(source), AX_X, ALU.add).then_inc(s_lsum, 1)
                dve.wait_ge(s_lsum, n + 1)
                nc.vector.tensor_scalar(ln_mean[:, :], ln_mean[:, :], 1.0 / CH, None, ALU.mult).then_inc(s_mean, 1)

            def variance(n):
                dve.wait_ge(s_sq, n + 1)
                nc.vector.tensor_reduce(ln_var[:, :], tch(left[:, AGG_T:AGG_T + ROW]), AX_X, ALU.add).then_inc(s_vsum, 1)
                dve.wait_ge(s_vsum, n + 1)
                nc.vector.tensor_scalar(ln_var[:, :], ln_var[:, :], 1.0 / CH, 1e-5, ALU.mult, ALU.add).then_inc(s_var, 1)

            def logits(b, j):
                dve.wait_ge(s_adjt[j % ADJT_SLOTS], 16 * (TILES // ADJT_SLOTS * b + j // ADJT_SLOTS + 1))
                if j == 0:
                    dve.wait_ge(s_drained, work_base(b) + W_SRC + 4)
                dve.sem_inc(s_begun, 1)
                a = adjt[j % ADJT_SLOTS][:, :]
                nc.vector.tensor_tensor_reduce(a, a, src_row[:, :], -0.8, 3.0e38, ALU.add, ALU.min,
                                               low[:, j:j + 1]).then_inc(s_t, 1)

            def masked(b, j, chunks):
                if j == 0 and 0 in chunks:
                    dve.wait_ge(s_drained, work_base(b) + W_DST + 2)
                for q in chunks:
                    dve.wait_ge(s_e, CHUNKS * (TILES * b + j) + q + 1)
                    a = adjt[j % ADJT_SLOTS][:, q * CHUNK:(q + 1) * CHUNK]
                    nc.vector.scalar_tensor_tensor(a, a, dst[:, j:j + 1], exps[:, (q % 2) * CHUNK:(q % 2 + 1) * CHUNK],
                                                   ALU.is_lt, ALU.mult,
                                                   part_sum[:, 4 * j + q:4 * j + q + 1]).then_inc(s_p, 1)

            def total(b, j):
                dve.wait_ge(s_p, CHUNKS * (TILES * b + j + 1))
                nc.vector.tensor_scalar(summed[:, :], part_sum[:, 4 * j:4 * j + 4], 1.0, TINY, ALU.mult, ALU.add,
                                        accum_out=total_sum[:, j:j + 1]).then_inc(s_z1, 1)

            def invert(b, j):
                dve.wait_ge(s_z1, TILES * b + j + 1)
                nc.vector.reciprocal(total_inv[:, j:j + 1], total_sum[:, j:j + 1]).then_inc(s_z, 1)

            def leaky(b):
                dve.wait_ge(s_drained, work_base(b) + W_HID + 2)
                h = left[:, LEAKY_T:LEAKY_T + ROW]
                nc.vector.scalar_tensor_tensor(h, h, 0.2, h, ALU.mult, ALU.max).then_inc(s_leaky, 1)

            def flags(b):
                dve.wait_ge(s_t, TILES * (b + 1))
                nc.vector.tensor_tensor(flag[:, :], low[:, :], dst[:, :], ALU.is_ge).then_inc(s_flag, 1)

            def step(b, l0, more):
                for j in range(1, TILES):
                    rows = ROWS_AT.get(j, []) if l0 else []
                    ended = [r - 2 for r in rows]
                    if j >= 2:
                        invert(b, j - 2)
                    if rows and ended[0] >= 0:
                        degree(b + 1, ended[0])
                    logits(b, j)
                    if rows[1:] and ended[1] >= 0:
                        degree(b + 1, ended[1])
                    if l0 and j == J_CENTER:
                        dve.wait_ge(s_x1, b + 2)
                        mean(2 * (b + 1) + 1, x1_next)
                    if j >= 2:
                        masked(b, j - 1, (0, 1))
                    if l0 and j == TILES - 1:
                        leaky(b + 1)
                    if l0 and j == J_NORM:
                        variance(2 * (b + 1) + 1)
                    if rows:
                        make_k(b + 1, K_IN.get(rows[0], []))
                    if j == TILES - 1:
                        flags(b)
                    masked(b, j - 1, (2, 3))
                    for r in rows[1:]:
                        make_k(b + 1, K_IN.get(r, []))
                    if more and j == J_NEXT:
                        dve.wait_ge(s_x, 16 * (b + 3))
                        mean(2 * (b + 2), x_in[:, :])
                    total(b, j - 1)
                invert(b, TILES - 2)
                masked(b, TILES - 1, (0, 1))
                if l0:
                    logits(b + 1, 0)
                masked(b, TILES - 1, (2, 3))
                total(b, TILES - 1)
                invert(b, TILES - 1)
                if more:
                    make_k(b + 2, [0])
                if l0:
                    masked(b + 1, 0, (0, 1))
                if more:
                    make_k(b + 2, [1])
                if more:
                    variance(2 * (b + 2))

            nc.vector.memset(src_row[:, :], 0.0).then_inc(s_zero, 1)
            dve.sem_inc(s_stored, 16)
            nc.vector.memset(uniform[:, :], 1.0 / NODES).then_inc(s_const, 1)
            dve.wait_ge(s_x, 16)
            mean(0, x_in[:, :])
            make_k(0, [0])
            variance(0)
            make_k(0, [1])
            for r in range(1, TILES + 2):
                if r >= 2:
                    degree(0, r - 2)
                make_k(0, K_IN.get(r, []))
            dve.wait_ge(s_x1, 1)
            mean(1, x1_next)
            variance(1)
            dve.wait_ge(s_x, 32)
            mean(2, x_in[:, :])
            make_k(1, [0])
            leaky(0)
            logits(0, 0)
            variance(2)
            masked(0, 0, (0, 1))
            make_k(1, [1])
            with dve.Fori(0, BATCH - 2) as b:
                step(b, True, True)
            step(BATCH - 2, True, False)
            step(BATCH - 1, False, False)

        @block.scalar
        def _(act):
            def left_row(b, r, turns):
                base = work_base(b) + TURN_AT[r]
                if r == 3 and not (isinstance(b, int) and b == 0):
                    act.wait_ge(s_stored, 16 * b)
                if r == 5 and not (isinstance(b, int) and b == 0):
                    act.wait_ge(s_x1m, b)
                for g in range(TURNS[r])[turns]:
                    w = (min(4 * g + 4, r) - 4 * g) * P
                    at = LEFT_AT[r % LEFTS] + g * CHUNK
                    k = TURN_AT[r] + g
                    act.wait_ge(s_filled, base + g + 1)
                    nc.scalar.activation(left[:, at:at + w], bank(k)[:, 0:w], ACT.Identity,
                                         accum_out=deg_part[:, 6 * r + 2 + g:6 * r + 3 + g]).then_inc(s_drained, 1)

            def scale_row(b, r):
                if r == 0:
                    act.wait_ge(s_norm, 2 * b + 1)
                act.wait_ge(s_deg, TILES * b + r + 1)
                if r >= 2:
                    act.wait_ge(s_mm0, TILES * b + r - 1)
                nc.scalar.activation(scaled[r % 2][:, :], x_norm[:, r * CH:(r + 1) * CH], ACT.Relu,
                                     scale=deg_inv[:, r:r + 1]).then_inc(s_scaled, 1)

            def row_begin(b, r):
                if r >= 2:
                    scale_row(b, r - 2)
                if r < TILES:
                    left_row(b, r, FIRST)

            def row_end(b, r):
                if r < TILES:
                    left_row(b, r, REST)

            def agg_out(b):
                act.wait_ge(s_mm0, TILES * (b + 1))
                nc.scalar.activation(left[:, AGG_T:AGG_T + ROW], acc0[:, :], ACT.Copy).then_inc(s_agg, 1)

            def to_nodes(dest, n_static, m):
                d = dest[:, m * HALF:(m + 1) * HALF].rearrange("p (h k c) -> p k h c", h=2, c=CH)
                s = bank(n_static).rearrange("p (k h c) -> p k h c", k=4, c=CH)
                return d, s

            def agg_back(b):
                for m in range(2):
                    act.wait_ge(s_filled, work_base(b) + W_AGG + m + 1)
                    d, s = to_nodes(x_norm, W_AGG + m, m)
                    nc.scalar.activation(d, s, ACT.Copy).then_inc(s_drained, 1)

            def square(n):
                act.wait_ge(s_cent, n + 1)
                nc.scalar.activation(left[:, AGG_T:AGG_T + ROW], x_norm[:, :], ACT.Square).then_inc(s_sq, 1)

            def activ_t(b):
                for m in range(2):
                    act.wait_ge(s_filled, work_base(b) + W_XN + m + 1)
                    nc.scalar.activation(left[:, ACTIV_T + m * HALF:ACTIV_T + (m + 1) * HALF], bank(W_XN + m),
                                         ACT.Relu).then_inc(s_drained, 1)

            def hidden_t_out(b):
                for m in range(2):
                    act.wait_ge(s_filled, work_base(b) + W_HID + m + 1)
                    nc.scalar.activation(left[:, LEAKY_T + m * HALF:LEAKY_T + (m + 1) * HALF], bank(W_HID + m),
                                         ACT.Copy).then_inc(s_drained, 1)

            def src_out(b, turns):
                if not (isinstance(b, int) and b == 0):
                    act.wait_ge(s_t, TILES * b)
                row = src_row[:, :].rearrange("p (q two n) -> p two q n", two=2, n=P)
                for k in turns:
                    act.wait_ge(s_filled, work_base(b) + W_SRC + k + 1)
                    nc.scalar.activation(row[:, k // 2, 4 * (k % 2):4 * (k % 2) + 4, :],
                                         bank(W_SRC + k).rearrange("p (q n) -> p q n", n=P), ACT.Copy,
                                         scale=0.25).then_inc(s_drained, 1)

            def dst_out(b):
                if not (isinstance(b, int) and b == 0):
                    act.wait_ge(s_p, CHUNKS * TILES * b)
                for m in range(2):
                    act.wait_ge(s_filled, work_base(b) + W_DST + m + 1)
                    nc.scalar.activation(dst[:, m * 8:(m + 1) * 8], bank(W_DST + m)[:, 0:8], ACT.Copy,
                                         scale=0.2).then_inc(s_drained, 1)

            def exponentials(b, j, chunks):
                act.wait_ge(s_t, TILES * b + j + 1)
                for q in chunks:
                    if j > 0 or q >= 2:
                        act.wait_ge(s_p, CHUNKS * (TILES * b + j) + q - 1)
                    nc.scalar.activation(exps[:, (q % 2) * CHUNK:(q % 2 + 1) * CHUNK],
                                         adjt[j % ADJT_SLOTS][:, q * CHUNK:(q + 1) * CHUNK], ACT.Exp,
                                         bias=low[:, j:j + 1], scale=-1.0).then_inc(s_e, 1)

            def weigh(b, j):
                if j == 0:
                    act.wait_ge(s_drained, work_base(b) + W_NAT + 2)
                act.wait_ge(s_z, TILES * b + j + 1)
                if j >= 2:
                    act.wait_ge(s_mm1, TILES * b + j - 1)
                nc.scalar.activation(weighed[j % 2][:, :], hidden[:, j * CH:(j + 1) * CH], ACT.Copy,
                                     scale=total_inv[:, j:j + 1]).then_inc(s_hz, 1)

            def acc1_out(b):
                act.wait_ge(s_acc1, b + 1)
                nc.scalar.activation(left[:, LEAKY_T:LEAKY_T + ROW], acc1[:, :], ACT.Copy).then_inc(s_hpt, 1)

            def hidden_out(b):
                for m in range(2):
                    act.wait_ge(s_filled, work_base(b) + W_NAT + m + 1)
                    nc.scalar.activation(hidden[:, m * HALF:(m + 1) * HALF], bank(W_NAT + m),
                                         ACT.Copy).then_inc(s_drained, 1)

            def relu_out(base, k):
                for m in range(2):
                    act.wait_ge(s_filled, base + k + m + 1)
                    d, s = to_nodes(left[:, AGG_T:AGG_T + ROW], k + m, m)
                    nc.scalar.activation(d, s, ACT.Relu).then_inc(s_drained, 1)

            def step(b, l0, more):
                for j in range(1, TILES):
                    rows = ROWS_AT.get(j, []) if l0 else []
                    if j >= 2:
                        weigh(b, j - 2)
                    if rows:
                        row_begin(b + 1, rows[0])
                    if j >= 2:
                        exponentials(b, j - 1, (2, 3))
                    if l0 and j == J_AGG:
                        agg_out(b + 1)
                    if l0 and j == J_TURN:
                        activ_t(b + 1)
                    if l0 and j == TILES - 1:
                        src_out(b + 1, (0, 1))
                    if rows:
                        row_end(b + 1, rows[0])
                    for r in rows[1:]:
                        row_begin(b + 1, r)
                    exponentials(b, j, (0, 1))
                    for r in rows[1:]:
                        row_end(b + 1, r)
                    if l0 and j == J_CENTER:
                        square(2 * (b + 1) + 1)
                    if l0 and j == J_TURN:
                        hidden_t_out(b + 1)
                    if l0 and j == J_AGG:
                        agg_back(b + 1)
                if l0:
                    src_out(b + 1, (2, 3))
                weigh(b, TILES - 2)
                exponentials(b, TILES - 1, (2, 3))
                weigh(b, TILES - 1)
                if l0:
                    dst_out(b + 1)
                if more:
                    square(2 * (b + 2))
                if l0:
                    exponentials(b + 1, 0, (0, 1))
                    exponentials(b + 1, 0, (2, 3))
                    act.wait_ge(s_lsm, b + 1)
                    hidden_out(b + 1)
                if more:
                    act.wait_ge(s_var, 2 * (b + 2) + 1)
                acc1_out(b)
                relu_out(work_base(b + 1), W_OUT if l0 else 0)

            k = 0
            for r in range(TILES):
                for c in range(r, TILES, 4):
                    w = (min(c + 4, TILES) - c) * P
                    act.wait_ge(s_filled, k + 1)
                    at = GATE_AT[r] + (c - r) * P
                    nc.scalar.activation(gate[:, at:at + w], gate_bank(k)[:, 0:w], ACT.Sigmoid).then_inc(s_drained, 1)
                    k += 1
                if r == 1:
                    square(0)
            for r in range(1, TILES + 2):
                row_begin(0, r)
                row_end(0, r)
            agg_out(0)
            agg_back(0)
            square(1)
            activ_t(0)
            hidden_t_out(0)
            src_out(0, range(4))
            dst_out(0)
            square(2)
            exponentials(0, 0, (0, 1))
            exponentials(0, 0, (2, 3))
            hidden_out(0)
            with act.Fori(0, BATCH - 2) as b:
                step(b, True, True)
            step(BATCH - 2, True, False)
            step(BATCH - 1, False, False)

        @block.tensor
        def _(pe):
            def free_bank(n):
                pe.wait_ge(s_drained, n - 1)

            def turn_row(b, r, turns):
                pe.wait_ge(s_k, len(UNITS) * b + UNITS_OF[r - 1][-1] + 1)
                for g in range(TURNS[r])[turns]:
                    k = TURN_AT[r] + g
                    free_bank(work_base(b) + k)
                    for c in range(4 * g, min(4 * g + 4, r)):
                        at = K_AT[c] + (r - c) * P
                        t = pe.transpose(bank(k)[:, (c % 4) * P:(c % 4 + 1) * P], k_rows[:, at:at + P], ident)
                    t.then_inc(s_filled, 1)

            def multiply_row(b, r, chunks):
                pe.wait_ge(s_scaled, TILES * b + r + 1)
                if r == 0 and not (isinstance(b, int) and b == 0):
                    pe.wait_ge(s_agg, b)
                for q in chunks:
                    lo, hi = q * CHUNK, (q + 1) * CHUNK
                    mid = min(max(r * P, lo), hi)
                    acc = chunk_of(acc0, q)
                    lw = scaled[r % 2][:, :]
                    parts = []
                    if lo < mid:
                        at = LEFT_AT[r % LEFTS]
                        parts.append((lo, mid, left[:, at + lo:at + mid]))
                    if mid < hi:
                        at = K_AT[r] - r * P
                        parts.append((mid, hi, k_rows[:, at + mid:at + hi]))
                    for n, (a, z, rhs) in enumerate(parts):
                        m = pe.matmul(acc[:, a - lo:z - lo], lw, rhs, start=(r == 0),
                                      stop=(r == TILES - 1 and n == len(parts) - 1))
                if CHUNKS - 1 in chunks:
                    m.then_inc(s_mm0, 1)

            def row(b, r, between=None):
                if r < TILES:
                    turn_row(b, r, FIRST)
                if between is not None:
                    between()
                elif r >= 2:
                    multiply_row(b, r - 2, (0, 1))
                if r < TILES and TURNS[r] > 2:
                    turn_row(b, r, REST)
                if r >= 2:
                    multiply_row(b, r - 2, range(CHUNKS) if between is not None else (2, 3))

            def turn_back(base, k0, region):
                for m in range(2):
                    free_bank(base + k0 + m)
                    for k in range(4):
                        at = region + (4 * m + k) * P
                        t = pe.transpose(bank(k0 + m)[:, k * P:(k + 1) * P], left[:, at:at + P], ident)
                    t.then_inc(s_filled, 1)

            def turn_norm(b):
                pe.wait_ge(s_norm, 2 * b + 2)
                for m in range(2):
                    free_bank(work_base(b) + W_XN + m)
                    for k in range(4):
                        q = 4 * m + k
                        t = pe.transpose(bank(W_XN + m)[:, k * P:(k + 1) * P], x_norm[:, q * P:(q + 1) * P], ident)
                    t.then_inc(s_filled, 1)

            def hidden_t(b):
                pe.wait_ge(s_drained, work_base(b) + W_XN + 2)
                for m in range(2):
                    free_bank(work_base(b) + W_HID + m)
                    pe.matmul(bank(W_HID + m), w_pair, left[:, ACTIV_T + m * HALF:ACTIV_T + (m + 1) * HALF],
                              start=True, stop=True).then_inc(s_filled, 1)

            def src_and_dst(b):
                pe.wait_ge(s_leaky, b + 1)
                for k in range(4):
                    free_bank(work_base(b) + W_SRC + k)
                    at = LEAKY_T + (k % 2) * HALF
                    pe.matmul(bank(W_SRC + k), cst[:, C_SRC + k // 2:C_SRC + k // 2 + 1].to_broadcast([P, P]),
                              left[:, at:at + HALF], start=True, stop=True).then_inc(s_filled, 1)
                for m in range(2):
                    free_bank(work_base(b) + W_DST + m)
                    for k in range(4):
                        at = LEAKY_T + (4 * m + k) * P
                        t = pe.matmul(bank(W_DST + m)[:, 2 * k:2 * k + 2], left[:, at:at + P],
                                      cst[:, C_DST:C_DST + 2], start=True, stop=True)
                    t.then_inc(s_filled, 1)

            def hidden_nodes(b):
                for m in range(2):
                    free_bank(work_base(b) + W_NAT + m)
                    for k in range(4):
                        at = ACTIV_T + (4 * m + k) * P
                        t = pe.matmul(bank(W_NAT + m)[:, k * P:(k + 1) * P], left[:, at:at + P], w_pair,
                                      start=True, stop=True)
                    t.then_inc(s_filled, 1)

            def gather_row(b, j):
                pe.wait_ge(s_hz, TILES * b + j + 1)
                for q in range(CHUNKS):
                    m = pe.matmul(chunk_of(acc1, q), weighed[j % 2][:, :],
                                  adjt[j % ADJT_SLOTS][:, q * CHUNK:(q + 1) * CHUNK], start=(j == 0), stop=False)
                m.then_inc(s_mm1, 1)

            def gather_lone(b):
                pe.wait_ge(s_lsm, b + 1)
                for q in range(CHUNKS):
                    m = pe.matmul(chunk_of(acc1, q), lone_sum[:, :], uniform[:, 0:1].to_broadcast([P, CHUNK]),
                                  start=False, stop=True)
                m.then_inc(s_acc1, 1)

            def step(b, l0, more):
                for j in range(1, TILES):
                    rows = ROWS_AT.get(j, []) if l0 else []
                    if l0 and j == J_TURN:
                        turn_norm(b + 1)
                    if l0 and j == TILES - 1:
                        src_and_dst(b + 1)
                    gather = (lambda: gather_row(b, j - 2)) if j >= 2 else None
                    if rows:
                        row(b + 1, rows[0], gather)
                    elif gather is not None:
                        gather()
                    for r in rows[1:]:
                        row(b + 1, r)
                    if l0 and j == J_AGG:
                        pe.wait_ge(s_agg, b + 2)
                        turn_back(work_base(b + 1), W_AGG, AGG_T)
                    if l0 and j == J_TURN:
                        hidden_t(b + 1)
                if l0:
                    hidden_nodes(b + 1)
                gather_row(b, TILES - 2)
                gather_row(b, TILES - 1)
                gather_lone(b)
                pe.wait_ge(s_hpt, b + 1)
                turn_back(work_base(b + 1), W_OUT if l0 else 0, LEAKY_T)

            pe.wait_ge(s_u, 16)
            k = 0
            for r in range(TILES):
                for c in range(r, TILES, 4):
                    w = (min(c + 4, TILES) - c) * P
                    if k >= 4:
                        pe.wait_ge(s_drained, k - 3)
                    pe.matmul(gate_bank(k)[:, 0:w], src_row[:, r * P:(r + 1) * P], src_row[:, c * P:c * P + w],
                              start=True, stop=True).then_inc(s_filled, 1)
                    k += 1
            pe.wait_ge(s_cst, 16)
            pe.wait_ge(s_const, 3)
            for r in range(1, TILES + 2):
                row(0, r)
            pe.wait_ge(s_agg, 1)
            turn_back(work_base(0), W_AGG, AGG_T)
            turn_norm(0)
            hidden_t(0)
            src_and_dst(0)
            hidden_nodes(0)
            with pe.Fori(0, BATCH - 2) as b:
                step(b, True, True)
            step(BATCH - 2, True, False)
            step(BATCH - 1, False, False)


def kernel(x, adj, L0_gnn_U, L0_gnn_w_scale, L1_gnn_W, L1_gnn_a):
    import concourse.bacc as bacc
    from concourse.bass_utils import run_bass_kernel_spmd

    x, adj, u, w_scale, w, a = (np.asarray(v) for v in (x, adj, L0_gnn_U, L0_gnn_w_scale, L1_gnn_W, L1_gnn_a))
    rows = np.ascontiguousarray(x.reshape(BATCH, TILES, P, CH).transpose(0, 2, 1, 3).reshape(BATCH, P, ROW))
    adj_t = np.ascontiguousarray(adj.transpose(0, 2, 1)).reshape(BATCH, TILES, P, NODES)
    tiled = adj.reshape(BATCH, TILES, P, NODES)
    pairs = np.empty((BATCH, P, PAIR_ROW), np.float32)
    for n, (r, c0, c1) in enumerate(UNITS):
        mid = (PAIR_AT[n] + PAIR_AT[n + 1]) // 2
        pairs[:, :, PAIR_AT[n]:mid] = tiled[:, r, :, c0 * P:c1 * P]
        pairs[:, :, mid:PAIR_AT[n + 1]] = adj_t[:, r, :, c0 * P:c1 * P]
    consts = np.zeros((P, C_COLS), np.float32)
    consts[:, C_ID:C_ID + P] = np.eye(P, dtype=np.float32)
    for half in range(2):
        at = slice(half * CH, (half + 1) * CH)
        consts[at, C_W + half * CH:C_W + (half + 1) * CH] = w
        consts[at, C_SRC + half] = a[:CH, 0]
        consts[at, C_DST + half] = a[CH:, 0]
    consts[:, C_SCALE] = w_scale
    arrays = {"x_rows": rows, "adj_pairs": pairs, "adj_t": adj_t, "u_t": np.ascontiguousarray(u.T), "consts": consts}
    nc = bacc.Bacc("TRN2", target_bir_lowering=False, num_devices=1, dynamic_dma_scratch_size=1024)
    aps = [nc.dram_tensor(name, v.shape, F32, kind="ExternalInput").ap() for name, v in arrays.items()]
    out = nc.dram_tensor("out_rows", (BATCH, P, ROW), F32, kind="ExternalOutput").ap()
    gnn_program(nc, *aps, out)
    got = run_bass_kernel_spmd(nc, [arrays], core_ids=[0]).results[0]["out_rows"]
    return np.ascontiguousarray(got.reshape(BATCH, P, TILES, CH).transpose(0, 2, 1, 3).reshape(BATCH, NODES, CH))
```
